# Optimizing a Trainium2 kernel written in Bass

```python
import numpy as np
import jax
import jax.numpy as jnp

def _softmax(x, axis=-1):
    return jax.nn.softmax(x, axis=axis)

def _gelu(x):
    return jax.nn.gelu(x, approximate=True)

def _silu(x):
    return jax.nn.silu(x)

def _sigmoid(x):
    return jax.nn.sigmoid(x)

def _layernorm(x, axis=-1, eps=1e-05):
    m = jnp.mean(x, axis=axis, keepdims=True)
    v = jnp.var(x, axis=axis, keepdims=True)
    return (x - m) / jnp.sqrt(v + eps)

def _scatter_add(tgt, idx, src, axis=0):
    return tgt.at[idx].add(src)

def _segment_sum(src, seg, n):
    return jax.ops.segment_sum(src, seg, n)
kernel_name = 'mk_adj_resnorm_d2_adj_r2_c7a9cb'

def setup_inputs(seed: int=0):
    np.random.seed(seed)
    _w = jnp.asarray

    def _rec_inputs():
        import jax
        import jax.numpy as jnp
        _gk = jax.random.key(seed)
        x = -0.000929 + 1 * jax.random.normal(jax.random.fold_in(_gk, 1), (4096, 128), jnp.float32)
        _a = jax.random.bernoulli(jax.random.fold_in(_gk, 2), 0.000488281, (4096, 4096))
        _af = _a.astype(jnp.float32)
        adj = _af
        return (x, adj)
    x, adj = _rec_inputs()

    def _L0_gnn_setup():
        import jax, jax.numpy as jnp
        import numpy as np
        N, IN_DIM, OUT_DIM, HEADS = (2048, 128, 128, 4)
        D_K = OUT_DIM // HEADS
        NEG_SLOPE = 0.2
        key = jax.random.key(seed)
        k1, k2, k3, k4, k5 = jax.random.split(key, 5)
        H = jax.random.normal(k1, (N, IN_DIM), dtype=jnp.float32)
        A = jax.random.randint(k2, (N, N), 0, 2).astype(jnp.float32)
        W = jax.random.normal(k3, (OUT_DIM, IN_DIM), dtype=jnp.float32) * (1.0 / np.sqrt(IN_DIM))
        a_l = jax.random.normal(k4, (HEADS, D_K), dtype=jnp.float32) * 0.1
        a_r = jax.random.normal(k5, (HEADS, D_K), dtype=jnp.float32) * 0.1
        return {'H': H, 'A': A, 'W': W, 'a_l': a_l, 'a_r': a_r}
    _L0_gnn_all = _L0_gnn_setup()
    _L0_gnn_in = {k: v for k, v in _L0_gnn_all.items() if k in ('W', 'a_l', 'a_r')}
    del _L0_gnn_all

    def _L1_gnn_setup():
        import jax, jax.numpy as jnp
        import numpy as np
        N, D_IN, D_OUT = (4096, 128, 128)
        key = jax.random.key(seed)
        k1, k2, k3, k4 = jax.random.split(key, 4)
        X = jax.random.normal(k1, (N, D_IN), dtype=jnp.float32)
        A = jax.random.uniform(k2, (N, N), dtype=jnp.float32)
        bound = float(np.sqrt(6.0 / (D_IN + D_OUT)))
        W = jax.random.uniform(k3, (D_OUT, D_IN), dtype=jnp.float32, minval=-bound, maxval=bound)
        b = jax.random.uniform(k4, (D_OUT,), dtype=jnp.float32, minval=-1.0 / np.sqrt(D_IN), maxval=1.0 / np.sqrt(D_IN))
        return {'X': X, 'A': A, 'W': W, 'b': b}
    _L1_gnn_all = _L1_gnn_setup()
    _L1_gnn_in = {k: v for k, v in _L1_gnn_all.items() if k in ('W', 'b')}
    del _L1_gnn_all
    return {'x': x, 'adj': adj, 'L0_gnn_W': _L0_gnn_in['W'], 'L0_gnn_a_l': _L0_gnn_in['a_l'], 'L0_gnn_a_r': _L0_gnn_in['a_r'], 'L1_gnn_W': _L1_gnn_in['W'], 'L1_gnn_b': _L1_gnn_in['b']}

def reference(x, adj, L0_gnn_W, L0_gnn_a_l, L0_gnn_a_r, L1_gnn_W, L1_gnn_b):
    import jax
    import jax.numpy as jnp

    def _L0_gnn_ref(H, A, W, a_l, a_r):
        import jax, jax.numpy as jnp
        import numpy as np
        N, IN_DIM, OUT_DIM, HEADS = (2048, 128, 128, 4)
        D_K = OUT_DIM // HEADS
        NEG_SLOPE = 0.2
        n = H.shape[0]
        A_tilde = A + jnp.eye(n, dtype=A.dtype)
        mask = A_tilde > 0
        Wh = (H @ W.T).reshape(n, HEADS, D_K)
        score_l = jnp.einsum('nhd,hd->nh', Wh, a_l)
        score_r = jnp.einsum('nhd,hd->nh', Wh, a_r)
        e = score_l[:, :, None] + score_r.T[None, :, :]
        e = jnp.where(e >= 0, e, NEG_SLOPE * e)
        e = jnp.where(mask[:, None, :], e, -jnp.inf)
        alpha = jax.nn.softmax(e, axis=2)
        out = jnp.einsum('nhm,mhd->nhd', alpha, Wh).reshape(n, OUT_DIM)
        return jax.nn.elu(out)

    def _L1_gnn_ref(X, A, W, b):
        import jax, jax.numpy as jnp
        import numpy as np
        N, D_IN, D_OUT = (4096, 128, 128)
        n = A.shape[0]
        A2 = A + 2.0 * jnp.eye(n, dtype=A.dtype)
        d = jnp.sum(A2, axis=1)
        dis = jax.lax.rsqrt(d)
        A_norm = A2 * dis[:, None] * dis[None, :]
        AX = A_norm @ X
        out = jax.nn.relu(AX @ W.T + b)
        return out
    x = _layernorm(x + _L0_gnn_ref(x, adj, L0_gnn_W, L0_gnn_a_l, L0_gnn_a_r), axis=-1)
    x = _layernorm(x + _L1_gnn_ref(x, adj, L1_gnn_W, L1_gnn_b), axis=-1)
    return x

_drawn_inputs = setup_inputs


def setup_inputs(seed=0):
    import zlib

    import numpy as np

    out = dict(_drawn_inputs(seed))
    spreads = {}
    factors = {}
    for name, (base, spread) in spreads.items():
        noise = np.random.default_rng([zlib.crc32(name.encode()), seed]).standard_normal(out[name].shape)
        drawn = base * np.exp(spread * noise) if base else spread * noise
        out[name] = jnp.asarray(drawn.astype(out[name].dtype))
    for name, factor in factors.items():
        out[name] = (out[name] * factor).astype(out[name].dtype)
    return out
```

```python
from contextlib import ExitStack

import concourse.bass as bass
from concourse import mybir

ALU = mybir.AluOpType
ACT = mybir.ActivationFunctionType
F32 = mybir.dt.float32
AX_X = mybir.AxisListType.X

P = 128
N = 4096
D = 128
HEADS = 4
DK = D // HEADS
BLOCKS = N // P
PANEL = 2
PANELS = BLOCKS // PANEL
NPAN = PANEL * P
TAB = D + 2 * HEADS
BANK = 512
FAR = 1.0e30
EPS = 1e-05
SLOPE = 0.2


def counter(eng, sem, per, turn):
    n = [0]

    def mark(*instructions):
        for ins in instructions:
            ins.then_inc(sem, 1)
            n[0] += 1

    def link(*instructions):
        mark(*instructions)
        eng.wait_ge(sem, per * turn + n[0])

    def taken():
        return n[0]

    return mark, link, taken


def build(nc, x_rows, x_cols, adj, adj_cols, w0, w0_t, a_l, a_r, w1_t, bias, out):
    with ExitStack() as ctx:
        def sb(name, shape, dt=F32):
            return ctx.enter_context(nc.sbuf_tensor(name, shape, dt))

        def sem(name):
            return ctx.enter_context(nc.semaphore(name))

        ident = sb("ident", [P, P])
        two_ident = sb("two_ident", [P, P])
        ones = sb("ones", [P, P])
        half_neg = sb("half_neg", [P, 2 * PANEL])
        x_sb = sb("x_sb", [P, BLOCKS, D])
        w0_sb = sb("w0_sb", [D, D])
        w1_sb = sb("w1_sb", [D, D])
        bias_row = sb("bias_row", [1, D])
        bias_sb = sb("bias_sb", [P, D])
        a_cols = sb("a_cols", [D, 2])
        a_heads = sb("a_heads", [D, 2 * HEADS])
        proj_w = sb("proj_w", [D, TAB])
        score_w = sb("score_w", [D, HEADS, P])
        table = sb("table", [P, BLOCKS, TAB])
        r_rows = sb("r_rows", [P, HEADS, N])
        adj_sb = sb("adj_sb", [P, N])
        pen = sb("pen", [P, N])
        scores = sb("scores", [P, 2, N])
        probs_t = sb("probs_t", [P, BLOCKS, P])
        hidden = sb("hidden", [P, BLOCKS, D])
        neg_max = sb("neg_max", [P, 4])
        denom = sb("denom", [P, BLOCKS, HEADS])
        degree = sb("degree", [P, BLOCKS])
        dis = sb("dis", [P, BLOCKS])
        work = sb("work", [P, 3, PANEL, D])
        small = sb("small", [P, 8 * PANEL])
        stats = sb("stats", [P, PANEL, 6])
        moments = sb("moments", [P, PANEL, 2])
        powers = sb("powers", [P, 2, 2 * PANEL])
        x_t = probs_t[:].rearrange("p b n -> p (b n)")
        scaled = probs_t
        panel = scores[:].rearrange("p s n -> p (s n)").rearrange("p (b n) -> p b n", b=BLOCKS)
        panel_agg = adj_sb[:, 0:NPAN]

        ps = ctx.enter_context(nc.psum_tensor("ps", [P, 8, BANK], F32))

        loaded = sem("loaded")
        constants = sem("constants")
        a_ready = sem("a_ready")
        score_w_done = sem("score_w_done")
        proj_w_ready = sem("proj_w_ready")
        score_w_ready = sem("score_w_ready")
        bias_done = sem("bias_done")
        proj_done = sem("proj_done")
        proj_saved = sem("proj_saved")
        rbc_done = sem("rbc_done")
        rbc_saved = sem("rbc_saved")

        adj_loaded = sem("adj_loaded")
        adj_used = sem("adj_used")
        vec_att = sem("vec_att")
        scores_ready = sem("scores_ready")
        scores_free = sem("scores_free")
        probs_ready = sem("probs_ready")
        transposed = sem("transposed")
        transposed_saved = sem("transposed_saved")
        group_summed = sem("group_summed")
        sums_done = sem("sums_done")
        sums_saved = sem("sums_saved")

        vec_gate = sem("vec_gate")
        vec_one = sem("vec_one")
        elu_in = sem("elu_in")
        elu_exp = sem("elu_exp")
        pow_in = sem("pow_in")
        pow_out = sem("pow_out")

        panel_loaded = sem("panel_loaded")
        diag_added = sem("diag_added")
        panel_summed = sem("panel_summed")
        agg_saved = sem("agg_saved")
        lin_done = sem("lin_done")
        vec_two = sem("vec_two")
        pow2_in = sem("pow2_in")
        pow2_out = sem("pow2_out")
        out_ready = sem("out_ready")
        out_free = sem("out_free")
        scaled_ready = sem("scaled_ready")
        out_stored = sem("out_stored")

        block = ctx.enter_context(nc.Block())

        @block.sync
        def _(sp):
            sp.dma_start(x_t, x_cols).then_inc(loaded, 16)
            sp.dma_start(proj_w[:, 0:D], w0_t).then_inc(loaded, 16)
            sp.dma_start(w0_sb[:], w0).then_inc(loaded, 16)
            sp.dma_start(a_cols[:, 0:1], a_l).then_inc(loaded, 16)
            sp.dma_start(a_cols[:, 1:2], a_r).then_inc(loaded, 16)
            sp.dma_start(bias_row[:], bias).then_inc(loaded, 16)
            sp.dma_start(w1_sb[:], w1_t).then_inc(loaded, 16)
            sp.dma_start(x_sb[:], x_rows.rearrange("(b p) d -> p b d", p=P)).then_inc(loaded, 16)
            sp.dma_start(adj_sb[:], adj[0:P, :]).then_inc(adj_loaded, 16)
            with sp.Fori(1, BLOCKS) as t:
                sp.wait_ge(adj_used, t)
                sp.dma_start(adj_sb[:], adj[bass.ds(t * P, P), :]).then_inc(adj_loaded, 16)
            sp.wait_ge(transposed, BLOCKS * HEADS * 8)
            sp.dma_start(panel, adj_cols[0]).then_inc(panel_loaded, 16)
            with sp.Fori(1, PANELS) as q:
                sp.wait_ge(panel_summed, q)
                sp.dma_start(panel, adj_cols[q]).then_inc(panel_loaded, 16)
            sp.wait_ge(out_stored, 16 * PANELS)

        @block.gpsimd
        def _(pool):
            nc.gpsimd.memset(ones[:], 1.0).then_inc(constants, 1)
            nc.gpsimd.memset(half_neg[:], -0.5).then_inc(constants, 1)
            pool.wait_ge(constants, 2)
            nc.gpsimd.affine_select(out=ident[:], in_=ones[:], compare_op=ALU.is_equal, fill=0.0, base=0,
                                    pattern=[[-1, P]], channel_multiplier=1).then_inc(constants, 1)
            with pool.Fori(0, PANELS) as q:
                pool.wait_ge(pow_in, 2 * q + 2)
                nc.gpsimd.tensor_tensor(powers[:, 1, :], powers[:, 0, :], half_neg[:], ALU.pow).then_inc(pow_out, 1)
            with pool.Fori(0, PANELS) as q:
                pool.wait_ge(pow2_in, q + 1)
                nc.gpsimd.tensor_tensor(powers[:, 1, 0:PANEL], powers[:, 0, 0:PANEL], half_neg[:, 0:PANEL],
                                        ALU.pow).then_inc(pow2_out, 1)

        @block.scalar
        def _(act):
            act.sem_inc(rbc_saved, 1)
            act.sem_inc(transposed_saved, 4)
            act.sem_inc(sums_saved, 1)
            act.sem_inc(out_free, 1)
            with act.Fori(0, BLOCKS // 4) as u:
                for k in range(4):
                    act.wait_ge(proj_done, 4 * u + k + 1)
                    nc.scalar.activation(table[:, bass.ds(4 * u + k, 1), :], ps[:, k:k + 1, 0:TAB],
                                         ACT.Copy).then_inc(proj_saved, 1)
            for k in range(HEADS):
                with act.Fori(0, N // BANK) as c:
                    act.wait_ge(rbc_done, k * (N // BANK) + c + 1)
                    nc.scalar.activation(r_rows[:, k, bass.ds(c * BANK, BANK)], ps[:, 7, :],
                                         ACT.Copy).then_inc(rbc_saved, 1)
            with act.Fori(0, BLOCKS) as t:
                for h in range(HEADS):
                    act.wait_ge(scores_ready, HEADS * t + h + 1)
                    nc.scalar.activation(scores[:, h % 2, :], scores[:, h % 2, :], ACT.Exp,
                                         bias=neg_max[:, h:h + 1],
                                         accum_out=denom[:, bass.ds(t, 1), h:h + 1]).then_inc(probs_ready, 1)
                    for g in range(8):
                        act.wait_ge(transposed, (HEADS * t + h) * 8 + g + 1)
                        act.wait_ge(group_summed, (HEADS * t + h) * 8 + g + 1)
                        nc.scalar.activation(probs_t[:, 4 * g:4 * g + 4, :],
                                             ps[:, g % 4, :].rearrange("p (b n) -> p b n", b=4),
                                             ACT.Copy).then_inc(transposed_saved, 1)
                act.wait_ge(sums_done, t + 1)
                nc.scalar.activation(hidden[:, bass.ds(t, 1), :], ps[:, 4:5, 0:D], ACT.Copy).then_inc(sums_saved, 1)
            with act.Fori(0, PANELS) as q:
                act.wait_ge(elu_in, q + 1)
                nc.scalar.activation(work[:, 1, :, :], work[:, 0, :, :], ACT.Exp).then_inc(elu_exp, 1)
            with act.Fori(0, PANELS) as q:
                act.wait_ge(panel_summed, q + 1)
                nc.scalar.activation(panel_agg, ps[:, 5, 0:NPAN], ACT.Copy).then_inc(agg_saved, 1)
                act.wait_ge(out_ready, PANEL * q + PANEL)
                act.dma_start(out.rearrange("(b p) d -> p b d", p=P)[:, bass.ds(PANEL * q, PANEL), :],
                              work[:, 2, :, :]).then_inc(out_stored, 16)
                act.wait_ge(out_stored, 16 * q + 16)
                act.sem_inc(out_free, 1)
            act.wait_ge(out_stored, 16 * PANELS)

        @block.vector
        def _(dve):
            nc.vector.memset(a_heads[:], 0.0).then_inc(a_ready, 1)
            dve.wait_ge(loaded, 16 * 8)
            dve.wait_ge(a_ready, 1)
            for h in range(HEADS):
                for s in range(2):
                    nc.vector.tensor_copy(a_heads[h * DK:(h + 1) * DK, s * HEADS + h:s * HEADS + h + 1],
                                          a_cols[h * DK:(h + 1) * DK, s:s + 1]).then_inc(a_ready, 1)
            dve.wait_ge(score_w_done, 1)
            nc.vector.tensor_copy(proj_w[:, D:TAB], ps[:, 5, 0:2 * HEADS]).then_inc(proj_w_ready, 1)
            dve.wait_ge(constants, 3)
            dve.wait_ge(proj_w_ready, 1)
            for h in range(HEADS):
                nc.vector.tensor_scalar(score_w[:, h, :], ones[:], proj_w[:, D + HEADS + h:D + HEADS + h + 1], None,
                                        ALU.mult).then_inc(score_w_ready, 1)
            nc.vector.tensor_scalar(two_ident[:], ident[:], 2.0, None, ALU.mult).then_inc(score_w_ready, 1)
            dve.wait_ge(bias_done, 1)
            nc.vector.tensor_copy(bias_sb[:], ps[:, 6, 0:D]).then_inc(score_w_ready, 1)
            dve.wait_ge(score_w_ready, HEADS + 2)
            dve.wait_ge(rbc_saved, HEADS * (N // BANK) + 1)
            dve.wait_ge(proj_saved, BLOCKS)

            PER = 3 + 3 * HEADS
            with dve.Fori(0, BLOCKS) as t:
                mark, link, taken = counter(dve, vec_att, PER, t)
                dve.wait_ge(adj_loaded, 16 * t + 16)
                diag = adj_sb[:, bass.ds(t * P, P)]
                link(nc.vector.tensor_tensor(diag, diag, ident[:], ALU.add))
                link(nc.vector.tensor_reduce(degree[:, bass.ds(t, 1)], adj_sb[:], AX_X, ALU.add),
                          nc.vector.tensor_scalar(pen[:], adj_sb[:], 0.0, -FAR, ALU.is_le, ALU.mult))
                dve.sem_inc(adj_used, 1)
                for h in range(HEADS):
                    s = scores[:, h % 2, :]
                    dve.wait_ge(scores_free, HEADS * t + h + 1)
                    link(nc.vector.tensor_scalar(s, r_rows[:, h, :], table[:, bass.ds(t, 1), D + h:D + h + 1],
                                                      None, ALU.add))
                    link(nc.vector.scalar_tensor_tensor(out=s, in0=s, scalar=SLOPE, in1=s, op0=ALU.mult,
                                                             op1=ALU.max))
                    dve.sem_inc(vec_gate, 1)
                    link(nc.vector.tensor_tensor_reduce(out=s, in0=s, in1=pen[:], scale=1.0, scalar=-3.0e38,
                                                             op0=ALU.add, op1=ALU.max, accum_out=small[:, h:h + 1]))
                    nc.vector.tensor_scalar(neg_max[:, h:h + 1], small[:, h:h + 1], -1.0, None,
                                            ALU.mult).then_inc(scores_ready, 1)
                assert taken() == PER

            dve.wait_ge(sums_saved, BLOCKS + 1)
            dve.wait_ge(scores_ready, BLOCKS * HEADS)
            PER = 3 + 8 * PANEL
            with dve.Fori(0, PANELS) as q:
                mark, link, taken = counter(dve, vec_one, PER, q)
                att = work[:, 2, :, :]
                for j in range(PANEL):
                    one = bass.ds(PANEL * q + j, 1)
                    r = small[:, j * HEADS:(j + 1) * HEADS]
                    link(nc.vector.reciprocal(r.unsqueeze(1), denom[:, one, :]))
                    link(*(nc.vector.tensor_scalar(work[:, 2, j:j + 1, h * DK:(h + 1) * DK],
                                                        hidden[:, one, h * DK:(h + 1) * DK],
                                                        r[:, h:h + 1], None, ALU.mult) for h in range(HEADS)))
                nc.vector.tensor_scalar(work[:, 0, :, :], att, 0.0, None, ALU.min).then_inc(elu_in, 1)
                dve.wait_ge(elu_exp, q + 1)
                link(nc.vector.scalar_tensor_tensor(out=att, in0=att, scalar=0.0, in1=work[:, 1, :, :],
                                                         op0=ALU.max, op1=ALU.add))
                link(nc.vector.scalar_tensor_tensor(out=att, in0=att, scalar=-1.0,
                                                         in1=x_sb[:, bass.ds(PANEL * q, PANEL), :],
                                                         op0=ALU.add, op1=ALU.add))
                link(*(nc.vector.bn_stats(stats[:, j, :], work[:, 2, j, :]) for j in range(PANEL)))
                dve.sem_inc(vec_gate, 1)
                link(*(nc.vector.bn_aggr(moments[:, j, :], stats[:, j, :]) for j in range(PANEL)))
                nc.vector.tensor_scalar(powers[:, 0, 0:PANEL], moments[:, :, 1], EPS, None,
                                        ALU.add).then_inc(pow_in, 1)
                nc.vector.tensor_scalar(powers[:, 0, PANEL:2 * PANEL], degree[:, bass.ds(PANEL * q, PANEL)], 1.0,
                                        None, ALU.add).then_inc(pow_in, 1)
                dve.wait_ge(pow_out, q + 1)
                for j in range(PANEL):
                    one = bass.ds(PANEL * q + j, 1)
                    mark(nc.vector.tensor_scalar(hidden[:, one, :], work[:, 2, j:j + 1, :],
                                                         moments[:, j, 0:1], powers[:, 1, j:j + 1],
                                                         ALU.subtract, ALU.mult))
                link(nc.vector.tensor_copy(dis[:, bass.ds(PANEL * q, PANEL)], powers[:, 1, PANEL:2 * PANEL]))
                for j in range(PANEL):
                    one = bass.ds(PANEL * q + j, 1)
                    nc.vector.tensor_scalar(scaled[:, one, :], hidden[:, one, :], powers[:, 1, PANEL + j:PANEL + j + 1],
                                            None, ALU.mult).then_inc(scaled_ready, 1)
                dve.wait_ge(scaled_ready, PANEL * q + PANEL)
                assert taken() == PER

            PER = 1 + 3 * PANEL
            with dve.Fori(0, PANELS) as q:
                mark, link, taken = counter(dve, vec_two, PER, q)
                dve.wait_ge(panel_loaded, 16 * q + 16)
                for j in range(PANEL):
                    d = panel[:, bass.ds(PANEL * q + j, 1), j * P:(j + 1) * P]
                    nc.vector.tensor_tensor(d, d, two_ident[:].unsqueeze(1), ALU.add).then_inc(diag_added, 1)
                dve.wait_ge(lin_done, q + 1)
                link(*(nc.vector.scalar_tensor_tensor(
                    out=work[:, 0, j, :], in0=ps[:, 6, j * D:(j + 1) * D], scalar=dis[:, bass.ds(PANEL * q + j, 1)],
                    in1=bias_sb[:], op0=ALU.mult, op1=ALU.add) for j in range(PANEL)))
                link(nc.vector.scalar_tensor_tensor(out=work[:, 1, :, :], in0=work[:, 0, :, :], scalar=0.0,
                                                         in1=hidden[:, bass.ds(PANEL * q, PANEL), :],
                                                         op0=ALU.max, op1=ALU.add))
                link(*(nc.vector.bn_stats(stats[:, j, :], work[:, 1, j, :]) for j in range(PANEL)))
                dve.sem_inc(vec_gate, 1)
                link(*(nc.vector.bn_aggr(moments[:, j, :], stats[:, j, :]) for j in range(PANEL)))
                nc.vector.tensor_scalar(powers[:, 0, 0:PANEL], moments[:, :, 1], EPS, None,
                                        ALU.add).then_inc(pow2_in, 1)
                dve.wait_ge(pow2_out, q + 1)
                dve.wait_ge(out_free, q + 1)
                for j in range(PANEL):
                    nc.vector.tensor_scalar(work[:, 2, j, :], work[:, 1, j, :], moments[:, j, 0:1],
                                            powers[:, 1, j:j + 1], ALU.subtract, ALU.mult).then_inc(out_ready, 1)
                dve.wait_ge(out_ready, PANEL * q + PANEL)
                assert taken() == PER

        @block.tensor
        def _(pe):
            pe.sem_inc(scores_free, 2)
            pe.sem_inc(group_summed, 8)
            pe.wait_ge(a_ready, 1 + 2 * HEADS)
            nc.tensor.matmul(ps[:, 5, 0:2 * HEADS], lhsT=w0_sb[:], rhs=a_heads[:], start=True,
                             stop=True).then_inc(score_w_done, 1)
            pe.wait_ge(constants, 3)
            nc.tensor.matmul(ps[:, 6, 0:D], lhsT=ones[0:1, :], rhs=bias_row[:], start=True,
                             stop=True).then_inc(bias_done, 1)
            pe.wait_ge(proj_w_ready, 1)
            for t in range(BLOCKS):
                if t >= 4:
                    pe.wait_ge(proj_saved, t - 3)
                nc.tensor.matmul(ps[:, t % 4, 0:TAB], lhsT=x_t[:, t * P:(t + 1) * P], rhs=proj_w[:], start=True,
                                 stop=True).then_inc(proj_done, 1)
            pe.wait_ge(score_w_ready, HEADS + 2)
            for h in range(HEADS):
                with pe.Fori(0, N // BANK) as c:
                    pe.wait_ge(rbc_saved, h * (N // BANK) + c + 1)
                    nc.tensor.matmul(ps[:, 7, :], lhsT=score_w[:, h, :], rhs=x_t[:, bass.ds(c * BANK, BANK)],
                                     start=True, stop=True).then_inc(rbc_done, 1)
            with pe.Fori(0, BLOCKS) as t:
                for h in range(HEADS):
                    pe.wait_ge(probs_ready, HEADS * t + h + 1)
                    for g in range(8):
                        pe.wait_ge(transposed_saved, (HEADS * t + h) * 8 + g + 1)
                        for b in range(4):
                            ins = nc.tensor.transpose(ps[:, g % 4, b * P:(b + 1) * P],
                                                      scores[:, h % 2, (4 * g + b) * P:(4 * g + b + 1) * P], ident[:])
                        ins.then_inc(transposed, 1)
                    if h == 0:
                        pe.wait_ge(sums_saved, t + 1)
                    for g in range(8):
                        pe.wait_ge(transposed_saved, (HEADS * t + h) * 8 + g + 5)
                        for b in range(4 * g, 4 * g + 4):
                            ins = nc.tensor.matmul(ps[:, 4, h * DK:(h + 1) * DK], lhsT=probs_t[:, b, :],
                                                   rhs=table[:, b, h * DK:(h + 1) * DK], start=(b == 0),
                                                   stop=(b == BLOCKS - 1))
                        ins.then_inc(group_summed, 1)
                    pe.wait_ge(group_summed, (HEADS * t + h) * 8 + 16)
                    pe.sem_inc(scores_free, 1)
                pe.sem_inc(sums_done, 1)
            pe.wait_ge(scaled_ready, BLOCKS)
            with pe.Fori(0, PANELS) as q:
                pe.wait_ge(diag_added, PANEL * q + PANEL)
                for b in range(BLOCKS):
                    ins = nc.tensor.matmul(ps[:, 5, 0:NPAN], lhsT=scaled[:, b, :], rhs=panel[:, b, :], start=(b == 0),
                                           stop=(b == BLOCKS - 1))
                ins.then_inc(panel_summed, 1)
                pe.wait_ge(agg_saved, q + 1)
                for j in range(PANEL):
                    ins = nc.tensor.matmul(ps[:, 6, j * D:(j + 1) * D], lhsT=panel_agg[:, j * P:(j + 1) * P],
                                           rhs=w1_sb[:], start=True, stop=True)
                ins.then_inc(lin_done, 1)


def kernel(x, adj, L0_gnn_W, L0_gnn_a_l, L0_gnn_a_r, L1_gnn_W, L1_gnn_b):
    import numpy as np
    import concourse.bacc as bacc
    from concourse.bass_utils import run_bass_kernel_spmd

    x, adj = np.asarray(x), np.asarray(adj)
    arrays = {
        "x_rows": x,
        "x_cols": x.T,
        "adj": adj,
        "adj_cols": adj.reshape(PANELS, NPAN, BLOCKS, P).transpose(0, 3, 2, 1),
        "w0": np.asarray(L0_gnn_W),
        "w0_t": np.asarray(L0_gnn_W).T,
        "a_l": np.asarray(L0_gnn_a_l).reshape(D, 1),
        "a_r": np.asarray(L0_gnn_a_r).reshape(D, 1),
        "w1_t": np.asarray(L1_gnn_W).T,
        "bias": np.asarray(L1_gnn_b).reshape(1, D),
    }
    arrays = {name: np.ascontiguousarray(a) for name, a in arrays.items()}
    nc = bacc.Bacc("TRN2", target_bir_lowering=False, num_devices=1)
    args = [nc.dram_tensor(name, a.shape, F32, kind="ExternalInput").ap() for name, a in arrays.items()]
    args.append(nc.dram_tensor("out", (N, D), F32, kind="ExternalOutput").ap())
    build(nc, *args)
    return run_bass_kernel_spmd(nc, [arrays], core_ids=[0]).results[0]["out"]
```

```python
from contextlib import ExitStack

import concourse.bass as bass
from concourse import mybir

ALU = mybir.AluOpType
ACT = mybir.ActivationFunctionType
F32 = mybir.dt.float32
F16 = mybir.dt.float16
BF16 = mybir.dt.bfloat16
I32 = mybir.dt.int32
U32 = mybir.dt.uint32
AX_X = mybir.AxisListType.X

P = 128
N = 4096
D = 128
HEADS = 4
DK = D // HEADS
BLOCKS = N // P
PANEL = 2
PANELS = BLOCKS // PANEL
NPAN = PANEL * P
TAB = D + 2 * HEADS
BANK = 512
FAR = 1.0e30
EPS = 1e-05
SLOPE = 0.2

BITS = 16
WORDS = N // BITS
BWORDS = P // BITS
LEVELS = 3
SLOTS = 16
CHUNKS = 5
WINDOW = [(0, 3), (1, 5)]
LOADS = 4
LBLOCKS = BLOCKS // LOADS
KEY_HI, KEY_LO, FIRST_HI, FIRST_LO, ROW, LEFT = 0, SLOTS, 2 * SLOTS, 2 * SLOTS + 1, 2 * SLOTS + 2, 2 * SLOTS + 3
SPREAD = LEFT + 3 * HEADS
C_IDENT = 0
C_BEFORE = C_IDENT + P
C_PACK = C_BEFORE + P
C_ROWS = C_PACK + BWORDS
C_EDGES = C_ROWS + NPAN
C_PLACE = C_EDGES + CHUNKS * P
C_SLOT = C_PLACE + CHUNKS
C_ROW = C_SLOT + SLOTS
C_BASE = C_ROW + BLOCKS
C_LOW = C_BASE + PANELS
C_HIGH = C_LOW + BLOCKS
CONSTS = C_HIGH + BLOCKS


def counter(eng, sem, per, turn):
    n = [0]

    def mark(*instructions):
        for ins in instructions:
            ins.then_inc(sem, 1)
            n[0] += 1

    def link(*instructions):
        mark(*instructions)
        eng.wait_ge(sem, per * turn + n[0])

    def taken():
        return n[0]

    return mark, link, taken


def wait(eng, sem, value):
    if not isinstance(value, int) or value > 0:
        eng.wait_ge(sem, value)


def sparse_path(nc, flag, table_rows, scaled_rows, consts, x_rows, x_cols, adj_cols, w0, w0_t, a_l, a_r, w1_t, bias,
                out):
    with ExitStack() as ctx:
        def sb(name, shape, dt=F32):
            return ctx.enter_context(nc.sbuf_tensor("s_" + name, shape, dt))

        def sem(name):
            return ctx.enter_context(nc.semaphore("s_" + name))

        cst = sb("cst", [P, CONSTS])
        ident, before = cst[:, C_IDENT:C_BEFORE], cst[:, C_BEFORE:C_PACK]
        two_ident = sb("two_ident", [P, P])
        ones_row = sb("ones_row", [1, P])
        pack_w = sb("pack_w", [P, BWORDS], BF16)
        before_w = sb("before_w", [P, P], BF16)
        ones_w = sb("ones_w", [P, P], BF16)
        edges = sb("edges", [P, CHUNKS * P], F16)
        eps = sb("eps", [P, 2])
        x_sb = sb("x_sb", [P, BLOCKS, D])
        w0_sb = sb("w0_sb", [D, D])
        w1_sb = sb("w1_sb", [D, D])
        bias_row = sb("bias_row", [1, D])
        bias_sb = sb("bias_sb", [P, D])
        a_cols = sb("a_cols", [D, 2])
        a_heads = sb("a_heads", [D, 2 * HEADS])
        proj_w = sb("proj_w", [D, TAB])
        table = sb("table", [P, BLOCKS, TAB])
        self_score = sb("self_score", [P, BLOCKS, HEADS])
        left_rest = sb("left_rest", [P, BLOCKS, HEADS])
        ring = sb("ring", [P, 2, LOADS, LBLOCKS * NPAN])
        x_t = ring[:].rearrange("p a b n -> p (a b n)")[:, 2 * LOADS * LBLOCKS * NPAN - N:]
        row_data = sb("row_data", [P, BLOCKS, SPREAD], BF16)
        degree = sb("degree", [P, BLOCKS])
        degree_w = sb("degree_w", [P, BLOCKS], BF16)
        first = sb("first", [P, BLOCKS])
        behind = sb("behind", [P, BLOCKS])
        found = sb("found", [P, BLOCKS])
        packed_sum = sb("packed_sum", [P, BLOCKS])
        last_key = sb("last_key", [P, BLOCKS])
        dis = sb("dis", [P, BLOCKS])
        all_idx = sb("all_idx", [P, PANELS, CHUNKS], I32)
        all_row = sb("all_row", [P, PANELS, CHUNKS])
        hidden = sb("hidden", [P, BLOCKS, D])
        scaled = sb("scaled", [P, BLOCKS, D])
        words_sb = sb("words_sb", [P, 2, PANEL, WORDS])
        top = sb("top", [P, LEVELS + 1, PANEL, SLOTS])
        where = sb("where", [P, PANEL, SLOTS], U32)
        word_key = sb("word_key", [P, PANEL, SLOTS])
        bit = sb("bit", [P, 2, PANEL, SLOTS], I32)
        key_tmp = sb("key_tmp", [P, PANEL, SLOTS])
        all_keys = sb("all_keys", [P, PANEL, LEVELS, SLOTS])
        rest_keys = sb("rest_keys", [P, PANEL, LEVELS * SLOTS])
        keys = sb("keys", [P, 2, PANEL, SLOTS])
        no_key = sb("no_key", [P, 2, PANEL, SLOTS])
        spread = sb("spread", [P, 2, PANEL, CHUNKS * P], BF16)
        from_first = sb("from_first", [P, PANEL, CHUNKS * P], BF16)
        edge_data = sb("edge_data", [P, 2, CHUNKS, SPREAD])
        edge_pos = sb("edge_pos", [P, 2, CHUNKS])
        edge_mask = sb("edge_mask", [P, 2, CHUNKS, SLOTS])
        edge_keys = sb("edge_keys", [P, CHUNKS, SLOTS])
        edge_key = sb("edge_key", [P, 2, CHUNKS])
        idx = sb("idx", [P, 2, CHUNKS], I32)
        gathered = sb("gathered", [P, 2, CHUNKS, TAB])
        select = sb("select", [P, 2, CHUNKS, NPAN])
        by_slot = sb("by_slot", [P, CHUNKS, SLOTS, HEADS])
        slot_r = sb("slot_r", [P, PANEL, SLOTS, HEADS])
        row_max = sb("row_max", [P, 2, PANEL, HEADS])
        shift = sb("shift", [P, 2, PANEL, HEADS])
        shift_parts = sb("shift_parts", [P, PANEL, 2 * HEADS], BF16)
        self_prob = sb("self_prob", [P, 2, PANEL, HEADS])
        edge_s = sb("edge_s", [P, 3, CHUNKS, HEADS])
        edge_p = sb("edge_p", [P, CHUNKS, HEADS])
        other = sb("other", [P, CHUNKS])
        att = sb("att", [P, 2, PANEL, D])
        att_exp = sb("att_exp", [P, PANEL, D])
        quotient = sb("quotient", [P, 2, PANEL, HEADS])
        stats = sb("stats", [P, PANEL, 6])
        moments = sb("moments", [P, PANEL, 2])
        log_var = sb("log_var", [P, PANEL])
        log_deg = sb("log_deg", [P, PANEL])
        rstd = sb("rstd", [P, PANEL])
        scaled_now = sb("scaled_now", [P, 2, PANEL, D])
        agg_cols = sb("agg_cols", [P, 2, NPAN])
        result = sb("result", [P, 2, PANEL, D])
        bad = sb("bad", [P, 6, BLOCKS])
        bad_row = sb("bad_row", [P, 1])

        ps_words = [ctx.enter_context(nc.psum_tensor(f"s_ps_words{i}", [P, PANEL, WORDS], F32)) for i in range(2)]
        ps_edge = ctx.enter_context(nc.psum_tensor("s_ps_edge", [P, CHUNKS, SPREAD], F32))
        ps_slot = ctx.enter_context(nc.psum_tensor("s_ps_slot", [P, PANEL, SLOTS * HEADS], F32))
        ps_small = ctx.enter_context(nc.psum_tensor("s_ps_small", [P, BANK], F32))
        ps_agg = ctx.enter_context(nc.psum_tensor("s_ps_agg", [P, BANK], F32))
        ps_agg2 = ctx.enter_context(nc.psum_tensor("s_ps_agg2", [P, BANK], F32))
        ps_first = ctx.enter_context(nc.psum_tensor("s_ps_first", [P, BANK], F32))
        ps_shift = ps_small[:, 0:CHUNKS * 2 * HEADS].rearrange("p (c h) -> p c h", c=CHUNKS)
        ps_att = ps_agg[:, 0:PANEL * (D + HEADS)].rearrange("p (j d) -> p j d", j=PANEL)
        ps_proj = [ps_agg, ps_agg2, ps_small, ps_first]

        consts_loaded, weights_loaded = sem("consts_loaded"), sem("weights_loaded")
        xcols_loaded, xrows_loaded = sem("xcols_loaded"), sem("xrows_loaded")
        set_up, heads_ready = sem("set_up"), sem("heads_ready")
        score_w_done, proj_w_ready = sem("score_w_done"), sem("proj_w_ready")
        bias_done = sem("bias_done")
        proj_done, proj_saved, table_stored = sem("proj_done"), sem("proj_saved"), sem("table_stored")
        vec_setup, rows_ready = sem("vec_setup"), sem("rows_ready")
        adj_loaded = [[sem(f"adj_loaded{i}{k}") for k in range(LOADS)] for i in range(2)]
        words_packed, words_summed, words_taken = sem("words_packed"), sem("words_summed"), sem("words_taken")
        pool_gate = sem("pool_gate")
        vec_gate, vec_find, vec_place, vec_index = sem("vec_gate"), sem("vec_find"), sem("vec_place"), sem("vec_index")
        counted, first_done, spread_ready = sem("counted"), sem("first_done"), sem("spread_ready")
        edges_spread, edges_saved, idx_ready = sem("edges_spread"), sem("edges_saved"), sem("idx_ready")
        rows_gathered = [sem(f"rows_gathered{i}") for i in range(2)]
        by_slot_ready, slots_done = sem("by_slot_ready"), sem("slots_done")
        vec_slot, vec_max, vec_score, vec_weight = sem("vec_slot"), sem("vec_max"), sem("vec_score"), sem("vec_weight")
        shift_ready, self_ready, shift_spread = sem("shift_ready"), sem("self_ready"), sem("shift_spread")
        self_exp, score_ready, score_exp = sem("self_exp"), sem("score_ready"), sem("score_exp")
        weighted, att_summed = sem("weighted"), sem("att_summed")
        vec_att, vec_norm, vec_layer = sem("vec_att"), sem("vec_norm"), sem("vec_layer")
        att_ready, att_exp_done = sem("att_ready"), sem("att_exp_done")
        act_stat, moments_ready, rstd_done = sem("act_stat"), sem("moments_ready"), sem("rstd_done")
        act_deg, dis_done = sem("act_deg"), sem("dis_done")
        scaled_ready, scaled_stored = sem("scaled_ready"), sem("scaled_stored")
        vec_flag, bad_ready, bad_summed, flag_set = sem("vec_flag"), sem("bad_ready"), sem("bad_summed"), sem("flag_set")
        idx2_ready, select2_ready = sem("idx2_ready"), sem("select2_ready")
        rows2_gathered = [sem(f"rows2_gathered{i}") for i in range(2)]
        now_ready, agg_done, agg_saved, lin_done = sem("now_ready"), sem("agg_done"), sem("agg_saved"), sem("lin_done")
        vec_two, lin_taken, select_ready = sem("vec_two"), sem("lin_taken"), sem("select_ready")
        act_stat2, moments2_ready, rstd2_done = sem("act_stat2"), sem("moments2_ready"), sem("rstd2_done")
        result_ready = sem("result_ready")
        result_stored = [sem(f"result_stored{i}") for i in range(2)]

        block = ctx.enter_context(nc.Block())

        def pipeline(eng, turn, behind):
            full = set(range(behind + 1))
            peeled = 4 if behind else 2
            for q in range(peeled):
                turn(q, q % 2, {k for k in full if q - k >= 0})
            with eng.Fori(peeled // 2, PANELS // 2) as u:
                for half in range(2):
                    turn(2 * u + half, half, full)
            for q in range(PANELS, PANELS + behind):
                turn(q, q % 2, {k for k in full if q - k < PANELS})

        def one(t):
            return bass.ds(t, 1)

        def tiles(q):
            return bass.ds(PANEL * q, PANEL)

        @block.sync
        def _(sp):
            sp.dma_start(x_t, x_cols).then_inc(xcols_loaded, 16)
            sp.dma_start(proj_w[:, 0:D], w0_t).then_inc(weights_loaded, 16)
            sp.dma_start(w0_sb[:], w0).then_inc(weights_loaded, 16)
            sp.dma_start(a_cols[:, 0:1], a_l).then_inc(weights_loaded, 16)
            sp.dma_start(a_cols[:, 1:2], a_r).then_inc(weights_loaded, 16)
            sp.dma_start(bias_row[:], bias).then_inc(weights_loaded, 16)
            sp.dma_start(w1_sb[:], w1_t).then_inc(weights_loaded, 16)
            sp.dma_start(cst[:], consts).then_inc(consts_loaded, 16)

            def load(q, half):
                for k in range(LOADS):
                    wait(sp, words_packed, LOADS * (q - 2) + k + 1)
                    sp.dma_start(ring[:, half, k, :].rearrange("p (b n) -> p b n", b=LBLOCKS),
                                 adj_cols[q, :, k * LBLOCKS:(k + 1) * LBLOCKS, :]).then_inc(adj_loaded[half][k], 16)

            load(0, 0)
            sp.dma_start(x_sb[:], x_rows.rearrange("(b p) d -> p b d", p=P)).then_inc(xrows_loaded, 16)
            sp.wait_ge(proj_done, BLOCKS)
            load(1, 1)
            with sp.Fori(1, PANELS // 2) as u:
                for half in range(2):
                    load(2 * u + half, half)

        @block.gpsimd
        def _(pool):
            def gather(source, width, indices, done, half):
                pool.sem_inc(pool_gate, 1)
                for c in range(CHUNKS):
                    pool.indirect_dma_start(
                        out=gathered[:, half, c, 0:width], out_offset=None, in_=source,
                        in_offset=bass.IndirectOffsetOnAxis(ap=indices[:, half, c:c + 1], axis=0)).then_inc(done, 16)

            pool.wait_ge(table_stored, 16)

            def turn(q, half, stages):
                pool.wait_ge(idx_ready, q + 1)
                wait(pool, att_summed, q - 1)
                gather(table_rows, TAB, idx, rows_gathered[half], half)

            pipeline(pool, turn, 0)
            pool.wait_ge(att_summed, PANELS)
            pool.wait_ge(scaled_stored, 16 * PANELS)

            def turn(q, half, stages):
                pool.wait_ge(idx2_ready, q + 1)
                wait(pool, agg_done, q - 1)
                gather(scaled_rows, D, idx, rows2_gathered[half], half)

            pipeline(pool, turn, 0)

        @block.tensor
        def _(pe):
            pe.wait_ge(heads_ready, 1 + 2 * HEADS)
            nc.tensor.matmul(ps_slot[:, 0, 0:2 * HEADS], lhsT=w0_sb[:], rhs=a_heads[:], start=True,
                             stop=True).then_inc(score_w_done, 1)
            pe.wait_ge(set_up, 1)
            nc.tensor.matmul(ps_edge[:].rearrange("p c s -> p (c s)")[:, 0:D], lhsT=ones_row[:], rhs=bias_row[:],
                             start=True, stop=True).then_inc(bias_done, 1)
            pe.wait_ge(proj_w_ready, 1)
            pe.wait_ge(xcols_loaded, 16)
            for t in range(BLOCKS):
                wait(pe, proj_saved, t - 3)
                nc.tensor.matmul(ps_proj[t % 4][:, 0:TAB], lhsT=x_t[:, t * P:(t + 1) * P], rhs=proj_w[:], start=True,
                                 stop=True).then_inc(proj_done, 1)
            pe.wait_ge(proj_saved, BLOCKS)
            pe.wait_ge(set_up, 9)

            def pack(q, half):
                for k in range(LOADS):
                    pe.wait_ge(adj_loaded[half][k], 8 * (q - half) + 16)
                    if k == 0:
                        wait(pe, words_summed, PANEL * (q - 1))
                    values = ring[:, half, k, :].bitcast(BF16).rearrange("p (b n two) -> p b n two", b=LBLOCKS, two=2)
                    for b in range(LBLOCKS):
                        w = (k * LBLOCKS + b) * BWORDS
                        for j in range(PANEL):
                            ins = nc.tensor.matmul(ps_words[half][:, j, w:w + BWORDS],
                                                   lhsT=values[:, b, j * P:(j + 1) * P, 1], rhs=pack_w[:],
                                                   start=True, stop=True)
                    ins.then_inc(words_packed, 1)

            def turn(q, half, stages):
                past = 1 - half
                if 0 in stages:
                    pack(q, half)
                    pe.wait_ge(counted, q + 1)
                    nc.tensor.matmul(ps_first[:, 0:PANEL], lhsT=before_w[:], rhs=degree_w[:, tiles(q)], start=True,
                                     stop=True)
                    for s in range(1, PANEL):
                        ins = nc.tensor.matmul(ps_first[:, s:PANEL], lhsT=ones_w[:],
                                               rhs=degree_w[:, bass.ds(PANEL * q, PANEL - s)], start=False,
                                               stop=True, skip_group_check=True)
                    ins.then_inc(first_done, 1)
                if 1 in stages:
                    pe.wait_ge(by_slot_ready, q)
                    pe.wait_ge(select_ready, CHUNKS * q)
                    for j in range(PANEL):
                        for c in range(*WINDOW[j]):
                            ins = nc.tensor.matmul(ps_slot[:, j, :], lhsT=select[:, past, c, j * P:(j + 1) * P],
                                                   rhs=by_slot[:, c, :, :].rearrange("p s h -> p (s h)"),
                                                   start=(c == WINDOW[j][0]), stop=(c == WINDOW[j][1] - 1))
                    ins.then_inc(slots_done, 1)
                if 0 in stages:
                    pe.wait_ge(spread_ready, PANEL * q + PANEL)
                    wait(pe, edges_saved, q)
                    for c in range(CHUNKS):
                        js = [j for j in range(PANEL) if c in range(*WINDOW[j])]
                        for j in js:
                            ins = nc.tensor.matmul(ps_edge[:, c, :], lhsT=spread[:, half, j, c * P:(c + 1) * P],
                                                   rhs=row_data[:, one(PANEL * q + j), :], start=(j == js[0]),
                                                   stop=(j == js[-1]))
                    ins.then_inc(edges_spread, 1)
                if 1 in stages:
                    pe.wait_ge(shift_ready, q)
                    for c in range(CHUNKS):
                        js = [j for j in range(PANEL) if c in range(*WINDOW[j])]
                        for j in js:
                            ins = nc.tensor.matmul(ps_shift[:, c, :], lhsT=spread[:, past, j, c * P:(c + 1) * P],
                                                   rhs=shift_parts[:, j, :], start=(j == js[0]), stop=(j == js[-1]))
                    ins.then_inc(shift_spread, 1)
                    pe.wait_ge(weighted, CHUNKS * q)
                    for j in range(PANEL):
                        for c in range(*WINDOW[j]):
                            ins = nc.tensor.matmul(ps_att[:, j, :], lhsT=select[:, past, c, j * P:(j + 1) * P],
                                                   rhs=gathered[:, past, c, 0:D + HEADS],
                                                   start=(c == WINDOW[j][0]), stop=(c == WINDOW[j][1] - 1))
                    ins.then_inc(att_summed, 1)

            pipeline(pe, turn, 1)
            pe.wait_ge(bad_ready, 1)
            nc.tensor.matmul(ps_first[0:1, 0:1], lhsT=bad_row[:], rhs=cst[:, C_ROW + 0:C_ROW + 1], start=True,
                             stop=True).then_inc(bad_summed, 1)

            def turn(q, half, stages):
                past = 1 - half
                if 0 in stages:
                    pe.wait_ge(now_ready, q + 1)
                    pe.wait_ge(select2_ready, CHUNKS * q + CHUNKS)
                    wait(pe, agg_saved, q - 1)
                    to = (ps_agg, ps_agg2)[half]
                    for j in range(PANEL):
                        nc.tensor.matmul(to[:, j * P:(j + 1) * P], lhsT=scaled_now[:, half, j, :], rhs=two_ident[:],
                                         start=(j == 0), stop=True, skip_group_check=True)
                    pe.wait_ge(rows2_gathered[half], 8 * CHUNKS * (q - half) + 16 * CHUNKS)
                    for c in range(CHUNKS):
                        js = [j for j in range(PANEL) if c in range(*WINDOW[j])]
                        cols = slice(js[0] * P, (js[-1] + 1) * P)
                        ins = nc.tensor.matmul(to[:, cols], lhsT=gathered[:, half, c, 0:D],
                                               rhs=select[:, half, c, cols], start=False, stop=True,
                                               skip_group_check=True)
                    ins.then_inc(agg_done, 1)
                if 1 in stages:
                    pe.wait_ge(agg_saved, q)
                    wait(pe, lin_taken, PANEL * (q - 1))
                    for j in range(PANEL):
                        ins = nc.tensor.matmul(ps_small[:, j * D:(j + 1) * D],
                                               lhsT=agg_cols[:, past, j * P:(j + 1) * P], rhs=w1_sb[:], start=True,
                                               stop=True)
                    ins.then_inc(lin_done, 1)

            pipeline(pe, turn, 1)

        @block.scalar
        def _(act):
            for t in range(BLOCKS):
                act.wait_ge(proj_done, t + 1)
                nc.scalar.activation(table[:, t, :], ps_proj[t % 4][:, 0:TAB], ACT.Copy).then_inc(proj_saved, 1)
            act.wait_ge(proj_saved, BLOCKS)
            act.dma_start(table_rows.rearrange("(b p) d -> p b d", p=P), table[:]).then_inc(table_stored, 16)
            act.wait_ge(set_up, 9)

            def turn(q, half, stages):
                past = 1 - half
                if 0 in stages:
                    act.wait_ge(words_packed, LOADS * q + LOADS)
                    wait(act, words_taken, q - 1)
                    for j in range(PANEL):
                        nc.scalar.activation(words_sb[:, half, j, :], ps_words[half][:, j, :], ACT.Copy,
                                             accum_out=packed_sum[:, one(PANEL * q + j)]).then_inc(words_summed, 1)
                if 2 in stages:
                    act.wait_ge(att_ready, PANEL * (q - 1))
                    nc.scalar.activation(att_exp[:], att[:, half, :, :], ACT.Exp).then_inc(att_exp_done, 1)
                if 0 in stages:
                    act.wait_ge(edges_spread, q + 1)
                    nc.scalar.activation(edge_data[:, half, :, :], ps_edge[:], ACT.Copy).then_inc(edges_saved, 1)
                    nc.scalar.activation(log_deg[:], degree[:, tiles(q)], ACT.Ln, bias=eps[:, 1:2]).then_inc(act_deg, 1)
                    act.wait_ge(act_deg, q + 1)
                    nc.scalar.activation(dis[:, tiles(q)], log_deg[:], ACT.Exp, scale=-0.5).then_inc(dis_done, 1)
                if 2 in stages:
                    act.wait_ge(moments_ready, PANEL * (q - 1))
                    nc.scalar.activation(log_var[:], moments[:, :, 1], ACT.Ln, bias=eps[:, 0:1]).then_inc(act_stat, 1)
                    act.wait_ge(act_stat, q - 1)
                    nc.scalar.activation(rstd[:], log_var[:], ACT.Exp, scale=-0.5).then_inc(rstd_done, 1)
                if 1 in stages:
                    act.wait_ge(self_ready, q)
                    nc.scalar.activation(self_prob[:, past, :, :], row_max[:, past, :, :], ACT.Exp)\
                        .then_inc(self_exp, 1)
                    act.wait_ge(score_ready, q)
                    nc.scalar.activation(edge_p[:], edge_s[:, 2, :, :], ACT.Exp).then_inc(score_exp, 1)
                if 2 in stages:
                    act.wait_ge(scaled_ready, PANEL * (q - 1))
                    act.dma_start(scaled_rows.rearrange("(b p) d -> p b d", p=P)[:, tiles(q - 2), :],
                                  scaled[:, tiles(q - 2), :]).then_inc(scaled_stored, 16)

            pipeline(act, turn, 2)

            def turn(q, half, stages):
                past = 1 - half
                if 0 in stages:
                    wait(act, agg_done, q - 1)
                    nc.scalar.activation(scaled_now[:, half, :, :], scaled[:, tiles(q), :], ACT.Copy)\
                        .then_inc(now_ready, 1)
                    act.wait_ge(agg_done, q + 1)
                    wait(act, lin_done, q - 1)
                    nc.scalar.activation(agg_cols[:, half, :], (ps_agg, ps_agg2)[half][:, 0:NPAN], ACT.Copy)\
                        .then_inc(agg_saved, 1)
                if 1 in stages:
                    act.wait_ge(moments2_ready, PANEL * q)
                    nc.scalar.activation(log_var[:], moments[:, :, 1], ACT.Ln, bias=eps[:, 0:1]).then_inc(act_stat2, 1)
                    act.wait_ge(act_stat2, q)
                    nc.scalar.activation(rstd[:], log_var[:], ACT.Exp, scale=-0.5).then_inc(rstd2_done, 1)
                    act.wait_ge(result_ready, PANEL * q)
                    act.dma_start(out.rearrange("(b p) d -> p b d", p=P)[:, tiles(q - 1), :],
                                  result[:, past, :, :]).then_inc(result_stored[past], 16)

            pipeline(act, turn, 1)
            for half in range(2):
                act.wait_ge(result_stored[half], 16 * PANELS // 2)

        @block.vector
        def _(dve):
            def gated():
                dve.sem_inc(vec_gate, 1)

            nc.vector.memset(a_heads[:], 0.0).then_inc(heads_ready, 1)
            nc.vector.memset(ones_row[:], 1.0).then_inc(set_up, 1)
            nc.vector.memset(ones_w[:], 1.0).then_inc(set_up, 1)
            nc.vector.memset(eps[:, 0:1], EPS).then_inc(set_up, 1)
            nc.vector.memset(eps[:, 1:2], 2.0).then_inc(set_up, 1)
            dve.wait_ge(weights_loaded, 16 * 6)
            dve.wait_ge(heads_ready, 1)
            for h in range(HEADS):
                for s in range(2):
                    nc.vector.tensor_copy(a_heads[h * DK:(h + 1) * DK, s * HEADS + h:s * HEADS + h + 1],
                                          a_cols[h * DK:(h + 1) * DK, s:s + 1]).then_inc(heads_ready, 1)
            dve.wait_ge(consts_loaded, 16)
            nc.vector.tensor_copy(pack_w[:], cst[:, C_PACK:C_ROWS]).then_inc(set_up, 1)
            nc.vector.tensor_copy(before_w[:], before).then_inc(set_up, 1)
            nc.vector.tensor_copy(edges[:], cst[:, C_EDGES:C_PLACE]).then_inc(set_up, 1)
            nc.vector.tensor_scalar(two_ident[:], ident, 2.0, None, ALU.mult).then_inc(set_up, 1)
            dve.wait_ge(score_w_done, 1)
            nc.vector.tensor_copy(proj_w[:, D:TAB], ps_slot[:, 0, 0:2 * HEADS]).then_inc(proj_w_ready, 1)
            dve.wait_ge(bias_done, 1)
            nc.vector.tensor_copy(bias_sb[:], ps_edge[:].rearrange("p c s -> p (c s)")[:, 0:D]).then_inc(set_up, 1)
            dve.wait_ge(proj_saved, BLOCKS)
            mark, link, taken = counter(dve, vec_setup, 0, 0)
            left, right = table[:, :, D:D + HEADS], table[:, :, D + HEADS:TAB]
            part = [row_data[:, :, LEFT + k * HEADS:LEFT + (k + 1) * HEADS] for k in range(3)]
            link(nc.vector.tensor_copy(row_data[:, :, ROW], cst[:, C_ROW:C_BASE]),
                 nc.vector.tensor_copy(part[0], left),
                 nc.vector.tensor_tensor(self_score[:], left, right, ALU.add))
            link(nc.vector.scalar_tensor_tensor(out=self_score[:], in0=self_score[:], scalar=SLOPE, in1=self_score[:],
                                                op0=ALU.mult, op1=ALU.max),
                 nc.vector.tensor_tensor(left_rest[:], left, part[0], ALU.subtract))
            link(nc.vector.tensor_copy(part[1], left_rest[:]))
            link(nc.vector.tensor_tensor(left_rest[:], left_rest[:], part[1], ALU.subtract))
            link(nc.vector.tensor_copy(part[2], left_rest[:]))

            def find(q, half):
                mark, link, taken = counter(dve, vec_find, FIND, q)
                words = words_sb[:, half, :, :]
                sides = [(j, s, words[:, j, s * WORDS // 2:(s + 1) * WORDS // 2]) for j in range(PANEL)
                         for s in range(2)]
                dve.wait_ge(words_summed, PANEL * q + PANEL)
                gated()
                link(*(nc.vector.max(top[:, 0, j, 8 * s:8 * s + 8], w) for j, s, w in sides))
                gated()
                mark(*(nc.vector.max_index(where[:, j, 8 * s:8 * s + 8], top[:, 0, j, 8 * s:8 * s + 8], w)
                       for j, s, w in sides))
                dve.wait_ge(vec_find, FIND * q + taken())
                dve.sem_inc(words_taken, 1)
                link(*(nc.vector.tensor_scalar(word_key[:, :, 8 * s:8 * s + 8], where[:, :, 8 * s:8 * s + 8],
                                               float(BITS), float(s * N // 2 + 1 - 127), ALU.mult, ALU.add)
                       for s in range(2)))
                for level in range(LEVELS):
                    v = top[:, level, :, :]
                    link(nc.vector.tensor_scalar(bit[:, 0, :, :], v.bitcast(I32), 23, None, ALU.logical_shift_right),
                         nc.vector.tensor_scalar(bit[:, 1, :, :], v.bitcast(I32), 0xFF << 23, None, ALU.bitwise_and))
                    link(nc.vector.tensor_tensor(key_tmp[:], bit[:, 0, :, :], word_key[:], ALU.add),
                         nc.vector.tensor_tensor(top[:, level + 1, :, :], v, bit[:, 1, :, :].bitcast(F32),
                                                 ALU.subtract))
                    link(nc.vector.scalar_tensor_tensor(out=all_keys[:, :, level, :], in0=v, scalar=0.0,
                                                        in1=key_tmp[:], op0=ALU.is_gt, op1=ALU.mult))
                link(nc.vector.tensor_tensor(key_tmp[:], top[:, 0, :, :], top[:, LEVELS, :, :], ALU.subtract))
                mark(nc.vector.tensor_reduce(found[:, tiles(q)], key_tmp[:], AX_X, ALU.add))
                every = [all_keys[:, j, :, :].rearrange("p l s -> p (l s)") for j in range(PANEL)]
                gated()
                link(*(nc.vector.max(keys[:, half, j, 0:8], every[j]) for j in range(PANEL)))
                gated()
                link(*(nc.vector.match_replace(rest_keys[:, j, :], keys[:, half, j, 0:8], every[j], 0.0)
                       for j in range(PANEL)))
                gated()
                link(*(nc.vector.max(keys[:, half, j, 8:16], rest_keys[:, j, :]) for j in range(PANEL)))
                k = keys[:, half, :, :]
                link(nc.vector.tensor_scalar(key_tmp[:], k, 0.0, None, ALU.is_gt),
                     nc.vector.tensor_scalar(no_key[:, half, :, :], k, 0.0, -FAR, ALU.is_le, ALU.mult),
                     nc.vector.tensor_copy(row_data[:, tiles(q), KEY_HI:KEY_HI + SLOTS], k),
                     nc.vector.tensor_copy(last_key[:, tiles(q)], k[:, :, SLOTS - 1]))
                mark(nc.vector.tensor_tensor(row_data[:, tiles(q), KEY_LO:KEY_LO + SLOTS], k,
                                             row_data[:, tiles(q), KEY_HI:KEY_HI + SLOTS], ALU.subtract))
                link(nc.vector.tensor_reduce(degree[:, tiles(q)], key_tmp[:], AX_X, ALU.add))
                nc.vector.tensor_copy(degree_w[:, tiles(q)], degree[:, tiles(q)]).then_inc(counted, 1)
                assert taken() == FIND, taken()

            def place(q, half):
                mark, link, taken = counter(dve, vec_place, PLACE, q)
                dve.wait_ge(first_done, q + 1)
                a = ps_first[:, 0:PANEL]
                link(nc.vector.tensor_copy(first[:, tiles(q)], a),
                     nc.vector.tensor_copy(row_data[:, tiles(q), FIRST_HI], a),
                     nc.vector.tensor_tensor(behind[:, tiles(q)], a, degree[:, tiles(q)], ALU.add))
                link(nc.vector.tensor_tensor(row_data[:, tiles(q), FIRST_LO], a, row_data[:, tiles(q), FIRST_HI],
                                             ALU.subtract),
                     *(nc.vector.tensor_scalar(from_first[:, j, WINDOW[j][0] * P:WINDOW[j][1] * P],
                                               edges[:, WINDOW[j][0] * P:WINDOW[j][1] * P],
                                               first[:, one(PANEL * q + j)], None, ALU.is_ge) for j in range(PANEL)))
                for j in range(PANEL):
                    e = slice(WINDOW[j][0] * P, WINDOW[j][1] * P)
                    ins = nc.vector.scalar_tensor_tensor(out=spread[:, half, j, e], in0=edges[:, e],
                                                         scalar=behind[:, one(PANEL * q + j)],
                                                         in1=from_first[:, j, e], op0=ALU.is_lt, op1=ALU.mult)
                    ins.then_inc(spread_ready, 1)
                assert taken() == PLACE, taken()

            def index(q, half):
                mark, link, taken = counter(dve, vec_index, INDEX, q)
                data = edge_data[:, half, :, :]
                wide = [P, CHUNKS, SLOTS]
                dve.wait_ge(edges_saved, q + 1)
                link(nc.vector.tensor_tensor(edge_pos[:, half, :], data[:, :, FIRST_HI], data[:, :, FIRST_LO], ALU.add),
                     nc.vector.tensor_tensor(edge_keys[:], data[:, :, KEY_HI:KEY_HI + SLOTS],
                                             data[:, :, KEY_LO:KEY_LO + SLOTS], ALU.add))
                link(nc.vector.tensor_tensor(edge_pos[:, half, :], cst[:, C_PLACE:C_SLOT], edge_pos[:, half, :],
                                             ALU.subtract))
                link(nc.vector.tensor_tensor(edge_mask[:, half, :, :],
                                             cst[:, C_SLOT:C_ROW].unsqueeze(1).to_broadcast(wide),
                                             edge_pos[:, half, :].unsqueeze(2).to_broadcast(wide), ALU.is_equal))
                link(nc.vector.tensor_tensor(edge_keys[:], edge_keys[:], edge_mask[:, half, :, :], ALU.mult))
                link(nc.vector.tensor_reduce(edge_key[:, half, :], edge_keys[:], AX_X, ALU.add))
                link(nc.vector.tensor_scalar(edge_pos[:, half, :], edge_key[:, half, :], 1.0, float(N), ALU.max,
                                             ALU.min))
                nc.vector.tensor_scalar(idx[:, half, :], edge_pos[:, half, :], -1.0, None, ALU.add)\
                    .then_inc(idx_ready, 1)
                mark(nc.vector.tensor_scalar(all_idx[:, one(q), :], edge_pos[:, half, :].unsqueeze(1), -1.0, None,
                                             ALU.add),
                     nc.vector.tensor_copy(all_row[:, one(q), :], data[:, :, ROW].unsqueeze(1)))
                assert taken() == INDEX, taken()

            def choose(q, half, row, sem_done):
                for c in range(CHUNKS):
                    js = [j for j in range(PANEL) if c in range(*WINDOW[j])]
                    nc.vector.tensor_scalar(select[:, half, c, js[0] * P:(js[-1] + 1) * P],
                                            cst[:, C_ROWS + js[0] * P:C_ROWS + (js[-1] + 1) * P], row(c), None,
                                            ALU.is_equal).then_inc(sem_done, 1)

            def slot(q, half):
                mark, link, taken = counter(dve, vec_slot, SLOT, q)
                data = edge_data[:, half, :, :]
                choose(q, half, lambda c: data[:, c, ROW:ROW + 1], select_ready)
                dve.wait_ge(rows_gathered[half], 8 * CHUNKS * (q - half) + 16 * CHUNKS)
                wide = [P, CHUNKS, SLOTS, HEADS]
                r = gathered[:, half, :, D + HEADS:TAB]
                nc.vector.tensor_tensor(by_slot[:], edge_mask[:, half, :, :].unsqueeze(3).to_broadcast(wide),
                                        r.unsqueeze(2).to_broadcast(wide), ALU.mult).then_inc(by_slot_ready, 1)
                s = edge_s[:, 0, :, :]
                left = [data[:, :, LEFT + k * HEADS:LEFT + (k + 1) * HEADS] for k in range(3)]
                link(nc.vector.tensor_tensor(s, left[0], left[1], ALU.add),
                     nc.vector.scalar_tensor_tensor(out=other[:], in0=data[:, :, ROW],
                                                    scalar=cst[:, bass.ds(q + C_BASE, 1)],
                                                    in1=edge_key[:, half, :], op0=ALU.add, op1=ALU.not_equal))
                link(nc.vector.tensor_tensor(s, s, left[2], ALU.add))
                link(nc.vector.tensor_tensor(s, s, r, ALU.add))
                mark(nc.vector.scalar_tensor_tensor(out=edge_s[:, 1, :, :], in0=s, scalar=SLOPE, in1=s, op0=ALU.mult,
                                                    op1=ALU.max))
                assert taken() == SLOT, taken()

            def greatest(q, half):
                mark, link, taken = counter(dve, vec_max, MAX, q)
                m = row_max[:, half, :, :]
                dve.wait_ge(slots_done, q + 1)
                link(nc.vector.tensor_tensor(slot_r[:], ps_slot[:].rearrange("p j (s h) -> p j s h", h=HEADS),
                                             no_key[:, half, :, :].unsqueeze(3).to_broadcast([P, PANEL, SLOTS, HEADS]),
                                             ALU.add))
                link(nc.vector.tensor_reduce(m, slot_r[:].rearrange("p j s h -> p j h s"), AX_X, ALU.max))
                link(nc.vector.tensor_tensor(m, m, table[:, tiles(q), D + HEADS:TAB], ALU.max))
                link(nc.vector.tensor_tensor(m, m, table[:, tiles(q), D:D + HEADS], ALU.add))
                link(nc.vector.scalar_tensor_tensor(out=m, in0=m, scalar=SLOPE, in1=m, op0=ALU.mult, op1=ALU.max))
                link(nc.vector.tensor_copy(shift_parts[:, :, 0:HEADS], m))
                nc.vector.tensor_tensor(shift_parts[:, :, HEADS:2 * HEADS], m, shift_parts[:, :, 0:HEADS],
                                        ALU.subtract).then_inc(shift_ready, 1)
                dve.wait_ge(shift_ready, q + 1)
                link(nc.vector.tensor_tensor(shift[:, half, :, :], shift_parts[:, :, 0:HEADS],
                                             shift_parts[:, :, HEADS:2 * HEADS], ALU.add))
                nc.vector.tensor_tensor(m, self_score[:, tiles(q), :], shift[:, half, :, :], ALU.subtract)\
                    .then_inc(self_ready, 1)
                assert taken() == MAX, taken()

            def score(q, half):
                mark, link, taken = counter(dve, vec_score, SCORE, q)
                dve.wait_ge(shift_spread, q + 1)
                dve.wait_ge(vec_slot, SLOT * q + SLOT)
                link(nc.vector.tensor_tensor(edge_s[:, 2, :, :], edge_s[:, 1, :, :], ps_shift[:, :, 0:HEADS],
                                             ALU.subtract))
                nc.vector.scalar_tensor_tensor(out=edge_s[:, 2, :, :], in0=edge_s[:, 2, :, :], scalar=60.0,
                                               in1=ps_shift[:, :, HEADS:2 * HEADS], op0=ALU.min, op1=ALU.subtract)\
                    .then_inc(score_ready, 1)
                assert taken() == SCORE, taken()

            def weigh(q, half):
                mark, link, taken = counter(dve, vec_weight, WEIGH, q)
                dve.wait_ge(score_exp, q + 1)
                link(nc.vector.tensor_tensor(gathered[:, half, :, D:D + HEADS], edge_p[:],
                                             other[:].unsqueeze(2).to_broadcast([P, CHUNKS, HEADS]), ALU.mult))
                rows = gathered[:, half, :, 0:D].rearrange("p c (h d) -> p c h d", h=HEADS)
                for c in range(CHUNKS):
                    nc.vector.tensor_tensor(
                        rows[:, c, :, :], rows[:, c, :, :],
                        gathered[:, half, c, D:D + HEADS].unsqueeze(2).to_broadcast([P, HEADS, DK]),
                        ALU.mult).then_inc(weighted, 1)
                assert taken() == WEIGH, taken()

            def attend(q, half):
                mark, link, taken = counter(dve, vec_att, ATT, q)
                wide = [P, HEADS, DK]
                a = att[:, half, :, :]
                dve.wait_ge(self_exp, q + 1)
                link(*(nc.vector.tensor_tensor(
                    a[:, j, :].rearrange("p (h d) -> p h d", h=HEADS),
                    table[:, one(PANEL * q + j), 0:D].rearrange("p a (h d) -> p (a h) d", h=HEADS),
                    self_prob[:, half, j, :].unsqueeze(2).to_broadcast(wide), ALU.mult) for j in range(PANEL)))
                dve.wait_ge(att_summed, q + 1)
                link(nc.vector.tensor_tensor(a, a, ps_att[:, :, 0:D], ALU.add),
                     nc.vector.tensor_tensor(quotient[:, 0, :, :], self_prob[:, half, :, :],
                                             ps_att[:, :, D:D + HEADS], ALU.add))
                link(nc.vector.reciprocal(quotient[:, 1, :, :], quotient[:, 0, :, :]))
                for j in range(PANEL):
                    heads = a[:, j, :].rearrange("p (h d) -> p h d", h=HEADS)
                    nc.vector.tensor_tensor(heads, heads, quotient[:, 1, j, :].unsqueeze(2).to_broadcast(wide),
                                            ALU.mult).then_inc(att_ready, 1)
                assert taken() == ATT, taken()

            def moment(q, half):
                mark, link, taken = counter(dve, vec_norm, NORM, q)
                a = att[:, half, :, :]
                dve.wait_ge(att_exp_done, q + 1)
                link(nc.vector.scalar_tensor_tensor(out=att_exp[:], in0=att_exp[:], scalar=1.0, in1=x_sb[:, tiles(q), :],
                                                    op0=ALU.min, op1=ALU.add))
                link(nc.vector.scalar_tensor_tensor(out=a, in0=a, scalar=0.0, in1=att_exp[:], op0=ALU.max,
                                                    op1=ALU.add))
                link(*(nc.vector.bn_stats(stats[:, j, :], a[:, j, :]) for j in range(PANEL)))
                gated()
                for j in range(PANEL):
                    nc.vector.bn_aggr(moments[:, j, :], stats[:, j, :]).then_inc(moments_ready, 1)
                assert taken() == NORM, taken()

            def layer(q, half):
                mark, link, taken = counter(dve, vec_layer, LAYER, q)
                dve.wait_ge(rstd_done, q + 1)
                dve.wait_ge(dis_done, q + 1)
                link(*(nc.vector.tensor_scalar(hidden[:, one(PANEL * q + j), :], att[:, half, j:j + 1, :],
                                               moments[:, j, 0:1], rstd[:, j:j + 1], ALU.subtract, ALU.mult)
                       for j in range(PANEL)))
                for j in range(PANEL):
                    nc.vector.tensor_scalar(scaled[:, one(PANEL * q + j), :], hidden[:, one(PANEL * q + j), :],
                                            dis[:, one(PANEL * q + j)], None, ALU.mult).then_inc(scaled_ready, 1)
                assert taken() == LAYER, taken()

            FIND, PLACE, INDEX, SLOT, MAX, SCORE, WEIGH, ATT, NORM, LAYER = \
                4 * PANEL + 2 + 5 * LEVELS + 2 + 3 * PANEL + 6, 4 + PANEL, 9, 5, 7, 1, 1, PANEL + 3, 2 + PANEL, PANEL

            dve.wait_ge(xrows_loaded, 16)

            def turn(q, half, stages):
                past = 1 - half
                if 0 in stages:
                    find(q, half)
                if 2 in stages:
                    attend(q - 2, half)
                if 1 in stages:
                    slot(q - 1, past)
                if 0 in stages:
                    place(q, half)
                if 2 in stages:
                    moment(q - 2, half)
                if 1 in stages:
                    greatest(q - 1, past)
                if 0 in stages:
                    index(q, half)
                if 1 in stages:
                    score(q - 1, past)
                if 2 in stages:
                    layer(q - 2, half)
                if 1 in stages:
                    weigh(q - 1, past)

            pipeline(dve, turn, 2)

            dve.wait_ge(words_summed, PANEL * PANELS)
            mark, link, taken = counter(dve, vec_flag, 0, 0)
            link(nc.vector.tensor_tensor(bad[:, 0, :], found[:], packed_sum[:], ALU.not_equal),
                 nc.vector.tensor_scalar(bad[:, 1, :], last_key[:], 0.0, None, ALU.is_gt),
                 nc.vector.tensor_tensor(bad[:, 2, :], first[:], cst[:, C_LOW:C_HIGH], ALU.is_lt),
                 nc.vector.tensor_tensor(bad[:, 3, :], behind[:], cst[:, C_HIGH:CONSTS], ALU.is_gt))
            nc.vector.tensor_reduce(bad_row[:], bad[:, 0:4, :].rearrange("p k t -> p (k t)"), AX_X, ALU.add)\
                .then_inc(bad_ready, 1)

            TWO = 1 + PANEL

            def bring(q, half):
                wait(dve, agg_done, q - 1)
                nc.vector.tensor_copy(idx[:, half:half + 1, :], all_idx[:, one(q), :]).then_inc(idx2_ready, 1)
                choose(q, half, lambda c: all_row[:, one(q), c:c + 1], select2_ready)

            def finish(q, half):
                mark, link, taken = counter(dve, vec_two, TWO, q)
                a = att[:, half, :, :]
                dve.wait_ge(lin_done, q + 1)
                for j in range(PANEL):
                    nc.vector.scalar_tensor_tensor(out=a[:, j:j + 1, :], in0=ps_small[:, j * D:(j + 1) * D].unsqueeze(1),
                                                   scalar=dis[:, one(PANEL * q + j)], in1=bias_sb[:].unsqueeze(1),
                                                   op0=ALU.mult, op1=ALU.add).then_inc(lin_taken, 1)
                dve.wait_ge(lin_taken, PANEL * q + PANEL)
                link(nc.vector.scalar_tensor_tensor(out=a, in0=a, scalar=0.0, in1=hidden[:, tiles(q), :],
                                                    op0=ALU.max, op1=ALU.add))
                link(*(nc.vector.bn_stats(stats[:, j, :], a[:, j, :]) for j in range(PANEL)))
                gated()
                for j in range(PANEL):
                    nc.vector.bn_aggr(moments[:, j, :], stats[:, j, :]).then_inc(moments2_ready, 1)
                dve.wait_ge(rstd2_done, q + 1)
                wait(dve, result_stored[half], 8 * (q - half))
                for j in range(PANEL):
                    nc.vector.tensor_scalar(result[:, half, j, :], a[:, j, :], moments[:, j, 0:1], rstd[:, j:j + 1],
                                            ALU.subtract, ALU.mult).then_inc(result_ready, 1)
                assert taken() == TWO, taken()

            def turn(q, half, stages):
                if 0 in stages:
                    bring(q, half)
                if 1 in stages:
                    finish(q - 1, 1 - half)
                if q == 0 if isinstance(q, int) else False:
                    dve.wait_ge(bad_summed, 1)
                    nc.vector.tensor_copy(flag[:], ps_first[0:1, 0:1]).then_inc(flag_set, 1)

            pipeline(dve, turn, 1)
            dve.wait_ge(flag_set, 1)


def general_path(nc, flag, x_rows, x_cols, adj, adj_cols, w0, w0_t, a_l, a_r, w1_t, bias, out):
    with ExitStack() as ctx:
        def sb(name, shape, dt=F32):
            return ctx.enter_context(nc.sbuf_tensor("g_" + name, shape, dt))

        def sem(name):
            return ctx.enter_context(nc.semaphore("g_" + name))

        ident = sb("ident", [P, P])
        two_ident = sb("two_ident", [P, P])
        ones = sb("ones", [P, P])
        half_neg = sb("half_neg", [P, 2 * PANEL])
        x_sb = sb("x_sb", [P, BLOCKS, D])
        w0_sb = sb("w0_sb", [D, D])
        w1_sb = sb("w1_sb", [D, D])
        bias_row = sb("bias_row", [1, D])
        bias_sb = sb("bias_sb", [P, D])
        a_cols = sb("a_cols", [D, 2])
        a_heads = sb("a_heads", [D, 2 * HEADS])
        proj_w = sb("proj_w", [D, TAB])
        score_w = sb("score_w", [D, HEADS, P])
        table = sb("table", [P, BLOCKS, TAB])
        r_rows = sb("r_rows", [P, HEADS, N])
        adj_sb = sb("adj_sb", [P, N])
        pen = sb("pen", [P, N])
        scores = sb("scores", [P, 2, N])
        probs_t = sb("probs_t", [P, BLOCKS, P])
        hidden = sb("hidden", [P, BLOCKS, D])
        neg_max = sb("neg_max", [P, 4])
        denom = sb("denom", [P, BLOCKS, HEADS])
        degree = sb("degree", [P, BLOCKS])
        dis = sb("dis", [P, BLOCKS])
        work = sb("work", [P, 3, PANEL, D])
        small = sb("small", [P, 8 * PANEL])
        stats = sb("stats", [P, PANEL, 6])
        moments = sb("moments", [P, PANEL, 2])
        powers = sb("powers", [P, 2, 2 * PANEL])
        x_t = probs_t[:].rearrange("p b n -> p (b n)")
        scaled = probs_t
        panel = scores[:].rearrange("p s n -> p (s n)").rearrange("p (b n) -> p b n", b=BLOCKS)
        panel_agg = adj_sb[:, 0:NPAN]

        ps = ctx.enter_context(nc.psum_tensor("g_ps", [P, 8, BANK], F32))

        loaded = sem("loaded")
        constants = sem("constants")
        a_ready = sem("a_ready")
        score_w_done = sem("score_w_done")
        proj_w_ready = sem("proj_w_ready")
        score_w_ready = sem("score_w_ready")
        bias_done = sem("bias_done")
        proj_done = sem("proj_done")
        proj_saved = sem("proj_saved")
        rbc_done = sem("rbc_done")
        rbc_saved = sem("rbc_saved")

        adj_loaded = sem("adj_loaded")
        adj_used = sem("adj_used")
        vec_att = sem("vec_att")
        scores_ready = sem("scores_ready")
        scores_free = sem("scores_free")
        probs_ready = sem("probs_ready")
        transposed = sem("transposed")
        transposed_saved = sem("transposed_saved")
        group_summed = sem("group_summed")
        sums_done = sem("sums_done")
        sums_saved = sem("sums_saved")

        vec_gate = sem("vec_gate")
        vec_one = sem("vec_one")
        elu_in = sem("elu_in")
        elu_exp = sem("elu_exp")
        pow_in = sem("pow_in")
        pow_out = sem("pow_out")

        panel_loaded = sem("panel_loaded")
        diag_added = sem("diag_added")
        panel_summed = sem("panel_summed")
        agg_saved = sem("agg_saved")
        lin_done = sem("lin_done")
        vec_two = sem("vec_two")
        pow2_in = sem("pow2_in")
        pow2_out = sem("pow2_out")
        out_ready = sem("out_ready")
        out_free = sem("out_free")
        scaled_ready = sem("scaled_ready")
        out_stored = sem("out_stored")

        block = ctx.enter_context(nc.Block())

        @block.sync
        def _(sp):
            with sp.If(sp.value_load(flag[0:1, 0:1]) != 0):
                sp.dma_start(x_t, x_cols).then_inc(loaded, 16)
                sp.dma_start(proj_w[:, 0:D], w0_t).then_inc(loaded, 16)
                sp.dma_start(w0_sb[:], w0).then_inc(loaded, 16)
                sp.dma_start(a_cols[:, 0:1], a_l).then_inc(loaded, 16)
                sp.dma_start(a_cols[:, 1:2], a_r).then_inc(loaded, 16)
                sp.dma_start(bias_row[:], bias).then_inc(loaded, 16)
                sp.dma_start(w1_sb[:], w1_t).then_inc(loaded, 16)
                sp.dma_start(x_sb[:], x_rows.rearrange("(b p) d -> p b d", p=P)).then_inc(loaded, 16)
                sp.dma_start(adj_sb[:], adj[0:P, :]).then_inc(adj_loaded, 16)
                with sp.Fori(1, BLOCKS) as t:
                    sp.wait_ge(adj_used, t)
                    sp.dma_start(adj_sb[:], adj[bass.ds(t * P, P), :]).then_inc(adj_loaded, 16)
                sp.wait_ge(transposed, BLOCKS * HEADS * 8)
                sp.dma_start(panel, adj_cols[0]).then_inc(panel_loaded, 16)
                with sp.Fori(1, PANELS) as q:
                    sp.wait_ge(panel_summed, q)
                    sp.dma_start(panel, adj_cols[q]).then_inc(panel_loaded, 16)
                sp.wait_ge(out_stored, 16 * PANELS)

        @block.gpsimd
        def _(pool):
            with pool.If(pool.value_load(flag[0:1, 0:1]) != 0):
                nc.gpsimd.memset(ones[:], 1.0).then_inc(constants, 1)
                nc.gpsimd.memset(half_neg[:], -0.5).then_inc(constants, 1)
                pool.wait_ge(constants, 2)
                nc.gpsimd.affine_select(out=ident[:], in_=ones[:], compare_op=ALU.is_equal, fill=0.0, base=0,
                                        pattern=[[-1, P]], channel_multiplier=1).then_inc(constants, 1)
                with pool.Fori(0, PANELS) as q:
                    pool.wait_ge(pow_in, 2 * q + 2)
                    nc.gpsimd.tensor_tensor(powers[:, 1, :], powers[:, 0, :], half_neg[:], ALU.pow).then_inc(pow_out, 1)
                with pool.Fori(0, PANELS) as q:
                    pool.wait_ge(pow2_in, q + 1)
                    nc.gpsimd.tensor_tensor(powers[:, 1, 0:PANEL], powers[:, 0, 0:PANEL], half_neg[:, 0:PANEL],
                                            ALU.pow).then_inc(pow2_out, 1)

        @block.scalar
        def _(act):
            with act.If(act.value_load(flag[0:1, 0:1]) != 0):
                act.sem_inc(rbc_saved, 1)
                act.sem_inc(transposed_saved, 4)
                act.sem_inc(sums_saved, 1)
                act.sem_inc(out_free, 1)
                with act.Fori(0, BLOCKS // 4) as u:
                    for k in range(4):
                        act.wait_ge(proj_done, 4 * u + k + 1)
                        nc.scalar.activation(table[:, bass.ds(4 * u + k, 1), :], ps[:, k:k + 1, 0:TAB],
                                             ACT.Copy).then_inc(proj_saved, 1)
                for k in range(HEADS):
                    with act.Fori(0, N // BANK) as c:
                        act.wait_ge(rbc_done, k * (N // BANK) + c + 1)
                        nc.scalar.activation(r_rows[:, k, bass.ds(c * BANK, BANK)], ps[:, 7, :],
                                             ACT.Copy).then_inc(rbc_saved, 1)
                with act.Fori(0, BLOCKS) as t:
                    for h in range(HEADS):
                        act.wait_ge(scores_ready, HEADS * t + h + 1)
                        nc.scalar.activation(scores[:, h % 2, :], scores[:, h % 2, :], ACT.Exp,
                                             bias=neg_max[:, h:h + 1],
                                             accum_out=denom[:, bass.ds(t, 1), h:h + 1]).then_inc(probs_ready, 1)
                        for g in range(8):
                            act.wait_ge(transposed, (HEADS * t + h) * 8 + g + 1)
                            act.wait_ge(group_summed, (HEADS * t + h) * 8 + g + 1)
                            nc.scalar.activation(probs_t[:, 4 * g:4 * g + 4, :],
                                                 ps[:, g % 4, :].rearrange("p (b n) -> p b n", b=4),
                                                 ACT.Copy).then_inc(transposed_saved, 1)
                    act.wait_ge(sums_done, t + 1)
                    nc.scalar.activation(hidden[:, bass.ds(t, 1), :], ps[:, 4:5, 0:D], ACT.Copy).then_inc(sums_saved, 1)
                with act.Fori(0, PANELS) as q:
                    act.wait_ge(elu_in, q + 1)
                    nc.scalar.activation(work[:, 1, :, :], work[:, 0, :, :], ACT.Exp).then_inc(elu_exp, 1)
                with act.Fori(0, PANELS) as q:
                    act.wait_ge(panel_summed, q + 1)
                    nc.scalar.activation(panel_agg, ps[:, 5, 0:NPAN], ACT.Copy).then_inc(agg_saved, 1)
                    act.wait_ge(out_ready, PANEL * q + PANEL)
                    act.dma_start(out.rearrange("(b p) d -> p b d", p=P)[:, bass.ds(PANEL * q, PANEL), :],
                                  work[:, 2, :, :]).then_inc(out_stored, 16)
                    act.wait_ge(out_stored, 16 * q + 16)
                    act.sem_inc(out_free, 1)
                act.wait_ge(out_stored, 16 * PANELS)

        @block.vector
        def _(dve):
            with dve.If(dve.value_load(flag[0:1, 0:1]) != 0):
                nc.vector.memset(a_heads[:], 0.0).then_inc(a_ready, 1)
                dve.wait_ge(loaded, 16 * 8)
                dve.wait_ge(a_ready, 1)
                for h in range(HEADS):
                    for s in range(2):
                        nc.vector.tensor_copy(a_heads[h * DK:(h + 1) * DK, s * HEADS + h:s * HEADS + h + 1],
                                              a_cols[h * DK:(h + 1) * DK, s:s + 1]).then_inc(a_ready, 1)
                dve.wait_ge(score_w_done, 1)
                nc.vector.tensor_copy(proj_w[:, D:TAB], ps[:, 5, 0:2 * HEADS]).then_inc(proj_w_ready, 1)
                dve.wait_ge(constants, 3)
                dve.wait_ge(proj_w_ready, 1)
                for h in range(HEADS):
                    nc.vector.tensor_scalar(score_w[:, h, :], ones[:], proj_w[:, D + HEADS + h:D + HEADS + h + 1], None,
                                            ALU.mult).then_inc(score_w_ready, 1)
                nc.vector.tensor_scalar(two_ident[:], ident[:], 2.0, None, ALU.mult).then_inc(score_w_ready, 1)
                dve.wait_ge(bias_done, 1)
                nc.vector.tensor_copy(bias_sb[:], ps[:, 6, 0:D]).then_inc(score_w_ready, 1)
                dve.wait_ge(score_w_ready, HEADS + 2)
                dve.wait_ge(rbc_saved, HEADS * (N // BANK) + 1)
                dve.wait_ge(proj_saved, BLOCKS)

                PER = 3 + 3 * HEADS
                with dve.Fori(0, BLOCKS) as t:
                    mark, link, taken = counter(dve, vec_att, PER, t)
                    dve.wait_ge(adj_loaded, 16 * t + 16)
                    diag = adj_sb[:, bass.ds(t * P, P)]
                    link(nc.vector.tensor_tensor(diag, diag, ident[:], ALU.add))
                    link(nc.vector.tensor_reduce(degree[:, bass.ds(t, 1)], adj_sb[:], AX_X, ALU.add),
                              nc.vector.tensor_scalar(pen[:], adj_sb[:], 0.0, -FAR, ALU.is_le, ALU.mult))
                    dve.sem_inc(adj_used, 1)
                    for h in range(HEADS):
                        s = scores[:, h % 2, :]
                        dve.wait_ge(scores_free, HEADS * t + h + 1)
                        link(nc.vector.tensor_scalar(s, r_rows[:, h, :], table[:, bass.ds(t, 1), D + h:D + h + 1],
                                                          None, ALU.add))
                        link(nc.vector.scalar_tensor_tensor(out=s, in0=s, scalar=SLOPE, in1=s, op0=ALU.mult,
                                                                 op1=ALU.max))
                        dve.sem_inc(vec_gate, 1)
                        link(nc.vector.tensor_tensor_reduce(out=s, in0=s, in1=pen[:], scale=1.0, scalar=-3.0e38,
                                                                 op0=ALU.add, op1=ALU.max, accum_out=small[:, h:h + 1]))
                        nc.vector.tensor_scalar(neg_max[:, h:h + 1], small[:, h:h + 1], -1.0, None,
                                                ALU.mult).then_inc(scores_ready, 1)
                    assert taken() == PER

                dve.wait_ge(sums_saved, BLOCKS + 1)
                dve.wait_ge(scores_ready, BLOCKS * HEADS)
                PER = 3 + 8 * PANEL
                with dve.Fori(0, PANELS) as q:
                    mark, link, taken = counter(dve, vec_one, PER, q)
                    att = work[:, 2, :, :]
                    for j in range(PANEL):
                        one = bass.ds(PANEL * q + j, 1)
                        r = small[:, j * HEADS:(j + 1) * HEADS]
                        link(nc.vector.reciprocal(r.unsqueeze(1), denom[:, one, :]))
                        link(*(nc.vector.tensor_scalar(work[:, 2, j:j + 1, h * DK:(h + 1) * DK],
                                                            hidden[:, one, h * DK:(h + 1) * DK],
                                                            r[:, h:h + 1], None, ALU.mult) for h in range(HEADS)))
                    nc.vector.tensor_scalar(work[:, 0, :, :], att, 0.0, None, ALU.min).then_inc(elu_in, 1)
                    dve.wait_ge(elu_exp, q + 1)
                    link(nc.vector.scalar_tensor_tensor(out=att, in0=att, scalar=0.0, in1=work[:, 1, :, :],
                                                             op0=ALU.max, op1=ALU.add))
                    link(nc.vector.scalar_tensor_tensor(out=att, in0=att, scalar=-1.0,
                                                             in1=x_sb[:, bass.ds(PANEL * q, PANEL), :],
                                                             op0=ALU.add, op1=ALU.add))
                    link(*(nc.vector.bn_stats(stats[:, j, :], work[:, 2, j, :]) for j in range(PANEL)))
                    dve.sem_inc(vec_gate, 1)
                    link(*(nc.vector.bn_aggr(moments[:, j, :], stats[:, j, :]) for j in range(PANEL)))
                    nc.vector.tensor_scalar(powers[:, 0, 0:PANEL], moments[:, :, 1], EPS, None,
                                            ALU.add).then_inc(pow_in, 1)
                    nc.vector.tensor_scalar(powers[:, 0, PANEL:2 * PANEL], degree[:, bass.ds(PANEL * q, PANEL)], 1.0,
                                            None, ALU.add).then_inc(pow_in, 1)
                    dve.wait_ge(pow_out, q + 1)
                    for j in range(PANEL):
                        one = bass.ds(PANEL * q + j, 1)
                        mark(nc.vector.tensor_scalar(hidden[:, one, :], work[:, 2, j:j + 1, :],
                                                             moments[:, j, 0:1], powers[:, 1, j:j + 1],
                                                             ALU.subtract, ALU.mult))
                    link(nc.vector.tensor_copy(dis[:, bass.ds(PANEL * q, PANEL)], powers[:, 1, PANEL:2 * PANEL]))
                    for j in range(PANEL):
                        one = bass.ds(PANEL * q + j, 1)
                        nc.vector.tensor_scalar(scaled[:, one, :], hidden[:, one, :], powers[:, 1, PANEL + j:PANEL + j + 1],
                                                None, ALU.mult).then_inc(scaled_ready, 1)
                    dve.wait_ge(scaled_ready, PANEL * q + PANEL)
                    assert taken() == PER

                PER = 1 + 3 * PANEL
                with dve.Fori(0, PANELS) as q:
                    mark, link, taken = counter(dve, vec_two, PER, q)
                    dve.wait_ge(panel_loaded, 16 * q + 16)
                    for j in range(PANEL):
                        d = panel[:, bass.ds(PANEL * q + j, 1), j * P:(j + 1) * P]
                        nc.vector.tensor_tensor(d, d, two_ident[:].unsqueeze(1), ALU.add).then_inc(diag_added, 1)
                    dve.wait_ge(lin_done, q + 1)
                    link(*(nc.vector.scalar_tensor_tensor(
                        out=work[:, 0, j, :], in0=ps[:, 6, j * D:(j + 1) * D], scalar=dis[:, bass.ds(PANEL * q + j, 1)],
                        in1=bias_sb[:], op0=ALU.mult, op1=ALU.add) for j in range(PANEL)))
                    link(nc.vector.scalar_tensor_tensor(out=work[:, 1, :, :], in0=work[:, 0, :, :], scalar=0.0,
                                                             in1=hidden[:, bass.ds(PANEL * q, PANEL), :],
                                                             op0=ALU.max, op1=ALU.add))
                    link(*(nc.vector.bn_stats(stats[:, j, :], work[:, 1, j, :]) for j in range(PANEL)))
                    dve.sem_inc(vec_gate, 1)
                    link(*(nc.vector.bn_aggr(moments[:, j, :], stats[:, j, :]) for j in range(PANEL)))
                    nc.vector.tensor_scalar(powers[:, 0, 0:PANEL], moments[:, :, 1], EPS, None,
                                            ALU.add).then_inc(pow2_in, 1)
                    dve.wait_ge(pow2_out, q + 1)
                    dve.wait_ge(out_free, q + 1)
                    for j in range(PANEL):
                        nc.vector.tensor_scalar(work[:, 2, j, :], work[:, 1, j, :], moments[:, j, 0:1],
                                                powers[:, 1, j:j + 1], ALU.subtract, ALU.mult).then_inc(out_ready, 1)
                    dve.wait_ge(out_ready, PANEL * q + PANEL)
                    assert taken() == PER

        @block.tensor
        def _(pe):
            with pe.If(pe.value_load(flag[0:1, 0:1]) != 0):
                pe.sem_inc(scores_free, 2)
                pe.sem_inc(group_summed, 8)
                pe.wait_ge(a_ready, 1 + 2 * HEADS)
                nc.tensor.matmul(ps[:, 5, 0:2 * HEADS], lhsT=w0_sb[:], rhs=a_heads[:], start=True,
                                 stop=True).then_inc(score_w_done, 1)
                pe.wait_ge(constants, 3)
                nc.tensor.matmul(ps[:, 6, 0:D], lhsT=ones[0:1, :], rhs=bias_row[:], start=True,
                                 stop=True).then_inc(bias_done, 1)
                pe.wait_ge(proj_w_ready, 1)
                for t in range(BLOCKS):
                    if t >= 4:
                        pe.wait_ge(proj_saved, t - 3)
                    nc.tensor.matmul(ps[:, t % 4, 0:TAB], lhsT=x_t[:, t * P:(t + 1) * P], rhs=proj_w[:], start=True,
                                     stop=True).then_inc(proj_done, 1)
                pe.wait_ge(score_w_ready, HEADS + 2)
                for h in range(HEADS):
                    with pe.Fori(0, N // BANK) as c:
                        pe.wait_ge(rbc_saved, h * (N // BANK) + c + 1)
                        nc.tensor.matmul(ps[:, 7, :], lhsT=score_w[:, h, :], rhs=x_t[:, bass.ds(c * BANK, BANK)],
                                         start=True, stop=True).then_inc(rbc_done, 1)
                with pe.Fori(0, BLOCKS) as t:
                    for h in range(HEADS):
                        pe.wait_ge(probs_ready, HEADS * t + h + 1)
                        for g in range(8):
                            pe.wait_ge(transposed_saved, (HEADS * t + h) * 8 + g + 1)
                            for b in range(4):
                                ins = nc.tensor.transpose(ps[:, g % 4, b * P:(b + 1) * P],
                                                          scores[:, h % 2, (4 * g + b) * P:(4 * g + b + 1) * P], ident[:])
                            ins.then_inc(transposed, 1)
                        if h == 0:
                            pe.wait_ge(sums_saved, t + 1)
                        for g in range(8):
                            pe.wait_ge(transposed_saved, (HEADS * t + h) * 8 + g + 5)
                            for b in range(4 * g, 4 * g + 4):
                                ins = nc.tensor.matmul(ps[:, 4, h * DK:(h + 1) * DK], lhsT=probs_t[:, b, :],
                                                       rhs=table[:, b, h * DK:(h + 1) * DK], start=(b == 0),
                                                       stop=(b == BLOCKS - 1))
                            ins.then_inc(group_summed, 1)
                        pe.wait_ge(group_summed, (HEADS * t + h) * 8 + 16)
                        pe.sem_inc(scores_free, 1)
                    pe.sem_inc(sums_done, 1)
                pe.wait_ge(scaled_ready, BLOCKS)
                with pe.Fori(0, PANELS) as q:
                    pe.wait_ge(diag_added, PANEL * q + PANEL)
                    for b in range(BLOCKS):
                        ins = nc.tensor.matmul(ps[:, 5, 0:NPAN], lhsT=scaled[:, b, :], rhs=panel[:, b, :], start=(b == 0),
                                               stop=(b == BLOCKS - 1))
                    ins.then_inc(panel_summed, 1)
                    pe.wait_ge(agg_saved, q + 1)
                    for j in range(PANEL):
                        ins = nc.tensor.matmul(ps[:, 6, j * D:(j + 1) * D], lhsT=panel_agg[:, j * P:(j + 1) * P],
                                               rhs=w1_sb[:], start=True, stop=True)
                    ins.then_inc(lin_done, 1)


def build(nc, consts, x_rows, x_cols, adj, adj_cols, w0, w0_t, a_l, a_r, w1_t, bias, out):
    table_rows = nc.dram_tensor("table_rows", (N, TAB), F32, kind="Internal").ap()
    scaled_rows = nc.dram_tensor("scaled_rows", (N, D), F32, kind="Internal").ap()
    with nc.sbuf_tensor("flag", [1, 1], I32) as flag:
        sparse_path(nc, flag, table_rows, scaled_rows, consts, x_rows, x_cols, adj_cols, w0, w0_t, a_l, a_r, w1_t,
                    bias, out)
        general_path(nc, flag, x_rows, x_cols, adj, adj_cols, w0, w0_t, a_l, a_r, w1_t, bias, out)


def layout_constants(np):
    c = np.zeros((P, CONSTS), np.float32)
    p = np.arange(P)
    c[:, C_IDENT:C_BEFORE] = np.eye(P)
    c[:, C_BEFORE:C_PACK] = p[:, None] < p
    c[p, C_PACK + p // BITS] = 2.0 ** (p % BITS)
    c[:, C_ROWS:C_EDGES] = 1 + np.arange(NPAN)
    c[:, C_EDGES:C_PLACE] = np.arange(CHUNKS * P)
    c[:, C_PLACE:C_SLOT] = P * np.arange(CHUNKS) + p[:, None]
    c[:, C_SLOT:C_ROW] = np.arange(SLOTS)
    c[:, C_ROW:C_BASE] = 1 + P * (np.arange(BLOCKS) % PANEL) + p[:, None]
    c[:, C_BASE:C_LOW] = NPAN * np.arange(PANELS)
    for t in range(BLOCKS):
        c[:, C_LOW + t] = P * WINDOW[t % PANEL][0]
        c[:, C_HIGH + t] = P * WINDOW[t % PANEL][1]
    return c


def kernel(x, adj, L0_gnn_W, L0_gnn_a_l, L0_gnn_a_r, L1_gnn_W, L1_gnn_b):
    import numpy as np
    import concourse.bacc as bacc
    from concourse.bass_utils import run_bass_kernel_spmd

    x, adj = np.asarray(x), np.asarray(adj)
    arrays = {
        "consts": layout_constants(np),
        "x_rows": x,
        "x_cols": x.T,
        "adj": adj,
        "adj_cols": adj.reshape(PANELS, NPAN, BLOCKS, P).transpose(0, 3, 2, 1),
        "w0": np.asarray(L0_gnn_W),
        "w0_t": np.asarray(L0_gnn_W).T,
        "a_l": np.asarray(L0_gnn_a_l).reshape(D, 1),
        "a_r": np.asarray(L0_gnn_a_r).reshape(D, 1),
        "w1_t": np.asarray(L1_gnn_W).T,
        "bias": np.asarray(L1_gnn_b).reshape(1, D),
    }
    arrays = {name: np.ascontiguousarray(a) for name, a in arrays.items()}
    nc = bacc.Bacc("TRN2", target_bir_lowering=False, num_devices=1)
    args = [nc.dram_tensor(name, a.shape, F32, kind="ExternalInput").ap() for name, a in arrays.items()]
    args.append(nc.dram_tensor("out", (N, D), F32, kind="ExternalOutput").ap())
    build(nc, *args)
    return run_bass_kernel_spmd(nc, [arrays], core_ids=[0]).results[0]["out"]
```

```python
from contextlib import ExitStack

import concourse.bass as bass
from concourse import mybir

ALU = mybir.AluOpType
ACT = mybir.ActivationFunctionType
F32 = mybir.dt.float32
F16 = mybir.dt.float16
BF16 = mybir.dt.bfloat16
I32 = mybir.dt.int32
U32 = mybir.dt.uint32
AX_X = mybir.AxisListType.X

P = 128
N = 4096
D = 128
HEADS = 4
DK = D // HEADS
BLOCKS = N // P
TAB = D + 2 * HEADS
BANK = 512
FAR = 1.0e30
EPS = 1e-05
SLOPE = 0.2

TILES = 4
PANELS = BLOCKS // TILES
ROWS = TILES * P
BITS = 16
WORDS = N // BITS
BWORDS = P // BITS
LEVELS = 3
SLOTS = 16
CHUNKS = 9
WINDOW = [(0, 3), (1, 5), (3, 7), (5, 9)]
WIDE = 4
TILES_OF = [[j for j in range(TILES) if WINDOW[j][0] <= c < WINDOW[j][1]] for c in range(CHUNKS)]
SPAN = max(len(ts) for ts in TILES_OF)
SHARE = 4
EARLY = 6
LOADS = 8
AHEAD = 3
LBLOCKS = BLOCKS // LOADS
BATCH = 3
KEY, FIRST, ROW, LEFT = 0, SLOTS, SLOTS + 1, SLOTS + 2
TAKEN = LEFT + HEADS
PARTS = 2 * TAKEN + HEADS
C_IDENT = 0
C_BEFORE = C_IDENT + P
C_PACK = C_BEFORE + P
C_PLACE = C_PACK + BWORDS
C_SLOT = C_PLACE + CHUNKS
C_ROW = C_SLOT + SLOTS
C_BASE = C_ROW + 2 * BLOCKS
C_LOW = C_BASE + PANELS
C_HIGH = C_LOW + BLOCKS
C_ROWS = C_HIGH + BLOCKS
C_EDGES = C_ROWS + ROWS
CONSTS = C_EDGES + CHUNKS * P
LINE = CONSTS - C_ROWS
PIECE = LINE // 4


def counter(eng, sem, per, turn):
    n = [0]

    def mark(*instructions):
        for ins in instructions:
            ins.then_inc(sem, 1)
            n[0] += 1

    def settle():
        eng.wait_ge(sem, per * turn + n[0])

    def link(*instructions):
        mark(*instructions)
        settle()

    def taken():
        return n[0]

    return mark, settle, link, taken


def wait(eng, sem, value):
    if not isinstance(value, int) or value > 0:
        eng.wait_ge(sem, value)


def alternate(*parts):
    parts = list(parts)
    while parts:
        for part in list(parts):
            if next(part, parts) is parts:
                parts.remove(part)


def later(turns, part):
    for _ in range(turns):
        yield
    yield from part


def in_turn(*parts):
    for part in parts:
        yield from part


def one(t):
    return bass.ds(t, 1)


def tiles(q):
    return bass.ds(TILES * q, TILES)


def sparse_path(nc, flag, table_rows, scaled_rows, consts, line, x_rows, adj_cols, w0, w0_t, a_l, a_r, w1_t, bias,
                out):
    with ExitStack() as ctx:
        def sb(name, shape, dt=F32):
            return ctx.enter_context(nc.sbuf_tensor("s_" + name, shape, dt))

        def psum(name, shape):
            return ctx.enter_context(nc.psum_tensor("s_" + name, shape, F32))

        def sem(name):
            return ctx.enter_context(nc.semaphore("s_" + name))

        cst = sb("cst", [P, CONSTS])
        two_ident = sb("two_ident", [P, P])
        ones_row = sb("ones_row", [1, P])
        pack_w = sb("pack_w", [P, BWORDS], BF16)
        before_w = sb("before_w", [P, P], BF16)
        ones_w = sb("ones_w", [P, P], BF16)
        eps = sb("eps", [P, 2])
        w0_sb = sb("w0_sb", [D, D])
        w1_sb = sb("w1_sb", [D, D])
        bias_row = sb("bias_row", [1, D])
        bias_sb = sb("bias_sb", [P, D])
        a_cols = sb("a_cols", [D, 2])
        a_heads = sb("a_heads", [D, 2 * HEADS])
        proj_w = sb("proj_w", [D, TAB])
        x_sb = sb("x_sb", [P, BLOCKS, D])
        table = sb("table", [P, BLOCKS, TAB])
        self_score = sb("self_score", [P, BLOCKS, HEADS])
        left_rest = sb("left_rest", [P, BLOCKS, HEADS])
        ring = sb("ring", [P, LOADS, LBLOCKS * ROWS])
        row_data = sb("row_data", [P, BLOCKS, PARTS], BF16)
        degree = sb("degree", [P, BLOCKS])
        degree_w = sb("degree_w", [P, BLOCKS], BF16)
        first = sb("first", [P, BLOCKS])
        behind = sb("behind", [P, BLOCKS])
        found = sb("found", [P, BLOCKS])
        packed_sum = sb("packed_sum", [P, BLOCKS])
        last_key = sb("last_key", [P, BLOCKS])
        dis = sb("dis", [P, BLOCKS])
        all_idx = sb("all_idx", [P, PANELS, CHUNKS], I32)
        all_row = sb("all_row", [P, PANELS, CHUNKS])
        hidden = sb("hidden", [P, BLOCKS, D])
        x_t = hidden[:].rearrange("p b d -> p (b d)")
        words_sb = sb("words_sb", [P, TILES, WORDS])
        top = sb("top", [P, LEVELS + 1, TILES, SLOTS])
        where = sb("where", [P, TILES, SLOTS], U32)
        word_key = sb("word_key", [P, TILES, SLOTS])
        bit = sb("bit", [P, 2, TILES, SLOTS], I32)
        key_tmp = sb("key_tmp", [P, LEVELS + 1, TILES, SLOTS])
        all_keys = sb("all_keys", [P, TILES, LEVELS, SLOTS])
        rest_keys = sb("rest_keys", [P, TILES, LEVELS * SLOTS])
        keys = sb("keys", [P, TILES, SLOTS])
        no_key = sb("no_key", [P, 2, TILES, SLOTS])
        off_middle = sb("off_middle", [P, TILES])
        distance = sb("distance", [P, TILES, WIDE * P], F16)
        spread = sb("spread", [P, 2, TILES, WIDE * P], BF16)
        edge_data = sb("edge_data", [P, 2, CHUNKS, TAKEN])
        edge_pos = sb("edge_pos", [P, CHUNKS])
        edge_mask = sb("edge_mask", [P, 2, CHUNKS, SLOTS])
        edge_keys = sb("edge_keys", [P, CHUNKS, SLOTS])
        edge_key = sb("edge_key", [P, 2, CHUNKS])
        idx = sb("idx", [P, 2, CHUNKS], I32)
        gathered = sb("gathered", [P, 2, CHUNKS, TAB])
        line_sb = gathered[0:1, :, :, :].rearrange("o k c d -> o (k c d)")[:, 0:LINE]
        select = sb("select", [P, 2, CHUNKS, SPAN * P])
        by_slot = sb("by_slot", [P, CHUNKS, SLOTS, HEADS])
        slot_r = sb("slot_r", [P, TILES, SLOTS, HEADS])
        row_max = sb("row_max", [P, 2, TILES, HEADS])
        shift = sb("shift", [P, TILES, HEADS])
        shift_parts = sb("shift_parts", [P, TILES, 2 * HEADS], BF16)
        self_prob = sb("self_prob", [P, 2, TILES, HEADS])
        edge_s = sb("edge_s", [P, 3, CHUNKS, HEADS])
        edge_p = sb("edge_p", [P, CHUNKS, HEADS])
        other = sb("other", [P, CHUNKS])
        att = sb("att", [P, 2, TILES, D])
        att_exp = sb("att_exp", [P, TILES, D])
        quotient = sb("quotient", [P, 2, TILES, HEADS])
        stats = sb("stats", [P, TILES, 6])
        moments = sb("moments", [P, TILES, 2])
        log_var = sb("log_var", [P, TILES])
        log_deg = sb("log_deg", [P, TILES])
        rstd = sb("rstd", [P, TILES])
        off_mean = sb("off_mean", [P, TILES])
        rstd_dis = sb("rstd_dis", [P, TILES])
        off_mean_dis = sb("off_mean_dis", [P, TILES])
        scaled = sb("scaled", [P, 2, TILES, D])
        agg_cols = sb("agg_cols", [P, ROWS])
        result = sb("result", [P, 2, TILES, D])
        bad = sb("bad", [P, 4, BLOCKS])
        bad_row = sb("bad_row", [P, 1])

        ps_words = psum("ps_words", [P, TILES, WORDS])
        ps_edge = psum("ps_edge", [P, BANK])
        ps_slot = psum("ps_slot", [P, BANK])
        ps_shift = psum("ps_shift", [P, BANK])
        ps_att = psum("ps_att", [P, 2, BANK])
        ps_first = psum("ps_first", [P, BANK])
        edge_out = ps_edge[:, 0:CHUNKS * TAKEN].rearrange("p (c s) -> p c s", c=CHUNKS)
        slot_out = ps_slot[:, 0:TILES * SLOTS * HEADS].rearrange("p (j k) -> p j k", j=TILES)
        shift_out = ps_shift[:, 0:CHUNKS * HEADS].rearrange("p (c h) -> p c h", c=CHUNKS)
        att_out = ps_att[:, :, 0:TILES // 2 * (D + HEADS)].rearrange("p k (j d) -> p k j d", k=2, j=TILES // 2)
        turn_out = [ps_edge, ps_slot]
        proj_out = [ps_att[:, 0, :], ps_att[:, 1, :], ps_shift[:], ps_first[:]]
        agg_out = [ps_att[:, 0, :], ps_att[:, 1, :]]
        lin_out = ps_shift

        consts_loaded, weights_loaded = sem("consts_loaded"), sem("weights_loaded")
        line_loaded, x_loaded = sem("line_loaded"), sem("x_loaded")
        line_spread, line_saved = sem("line_spread"), sem("line_saved")
        x_turned, x_t_saved = sem("x_turned"), sem("x_t_saved")
        set_up, heads_ready, ones_ready = sem("set_up"), sem("heads_ready"), sem("ones_ready")
        bias_saved = sem("bias_saved")
        score_w_done, proj_w_ready, bias_done = sem("score_w_done"), sem("proj_w_ready"), sem("bias_done")
        proj_done, proj_saved, table_stored = sem("proj_done"), sem("proj_saved"), sem("table_stored")
        adj_loaded = [sem(f"adj_loaded{k}") for k in range(LOADS)]
        words_packed, words_summed, words_taken = sem("words_packed"), sem("words_summed"), sem("words_taken")
        vec_setup, vec_gate, pool_gate = sem("vec_setup"), sem("vec_gate"), sem("pool_gate")
        load_gate = sem("load_gate")
        vec_find, vec_place, vec_index = sem("vec_find"), sem("vec_place"), sem("vec_index")
        counted, first_done = sem("counted"), sem("first_done")
        middle_ready, distance_ready, spread_ready = sem("middle_ready"), sem("distance_ready"), sem("spread_ready")
        edges_spread, edges_saved, idx_ready = sem("edges_spread"), sem("edges_saved"), sem("idx_ready")
        rows_gathered = [sem(f"rows_gathered{i}") for i in range(2)]
        vec_slot, vec_max, vec_weight = sem("vec_slot"), sem("vec_max"), sem("vec_weight")
        share_ready = sem("share_ready")
        select_ready, by_slot_ready, slots_done = sem("select_ready"), sem("by_slot_ready"), sem("slots_done")
        shift_ready, self_ready, shift_spread = sem("shift_ready"), sem("self_ready"), sem("shift_spread")
        self_exp, score_ready, score_exp = sem("self_exp"), sem("score_ready"), sem("score_exp")
        weighted, att_summed = sem("weighted"), sem("att_summed")
        vec_att, vec_norm = sem("vec_att"), sem("vec_norm")
        att_ready, att_exp_done = sem("att_ready"), sem("att_exp_done")
        act_stat, moments_ready, rstd_done = sem("act_stat"), sem("moments_ready"), sem("rstd_done")
        act_deg, dis_done = sem("act_deg"), sem("dis_done")
        mean_ready, hidden_ready, scaled_ready = sem("mean_ready"), sem("hidden_ready"), sem("scaled_ready")
        scaled_free = [sem(f"scaled_free{i}") for i in range(2)]
        vec_flag, bad_ready, bad_summed, flag_set = sem("vec_flag"), sem("bad_ready"), sem("bad_summed"), sem("flag_set")
        idx2_ready, select2_ready = sem("idx2_ready"), sem("select2_ready")
        rows2_gathered = [sem(f"rows2_gathered{i}") for i in range(2)]
        rows2_late = [sem(f"rows2_late{i}") for i in range(2)]
        now_ready, agg_done, agg_saved, lin_done = sem("now_ready"), sem("agg_done"), sem("agg_saved"), sem("lin_done")
        vec_two, lin_taken = sem("vec_two"), sem("lin_taken")
        act_stat2, moments2_ready, rstd2_done = sem("act_stat2"), sem("moments2_ready"), sem("rstd2_done")
        mean2_ready, result_ready = sem("mean2_ready"), sem("result_ready")
        result_stored = [sem(f"result_stored{i}") for i in range(2)]

        block = ctx.enter_context(nc.Block())

        def pipeline(eng, turn, stages):
            peeled = 4 if stages > 1 else 2
            for q in range(peeled):
                turn(q, q % 2, [k for k in range(stages) if q - k >= 0])
            with eng.Fori(peeled // 2, PANELS // 2) as u:
                for half in range(2):
                    turn(2 * u + half, half, list(range(stages)))
            for q in range(PANELS, PANELS + stages - 1):
                turn(q, q % 2, [k for k in range(stages) if q - k < PANELS])

        def choose(eng, half, c, row, done):
            lo, hi = TILES_OF[c][0] * P, (TILES_OF[c][-1] + 1) * P
            eng.tensor_scalar(select[:, half, c, 0:hi - lo], cst[:, C_ROWS + lo:C_ROWS + hi], row, None, ALU.is_equal)\
                .then_inc(done, 1)

        @block.sync
        def _(sp):
            def load(q, k):
                wait(sp, words_packed, LOADS * (q - 1) + k + 1)
                sp.sem_inc(load_gate, 1)
                wait(sp, adj_loaded[(k - AHEAD) % LOADS], 16 * q + 16 * (k >= AHEAD))
                sp.dma_start(ring[:, k, :].rearrange("p (b n) -> p b n", b=LBLOCKS),
                             adj_cols[q, :, k * LBLOCKS:(k + 1) * LBLOCKS, :]).then_inc(adj_loaded[k], 16)

            sp.dma_start(line_sb, line).then_inc(line_loaded, 16)
            sp.dma_start(cst[:, 0:C_ROWS], consts).then_inc(consts_loaded, 16)
            for k in range(AHEAD):
                load(0, k)
            sp.dma_start(w0_sb[:], w0).then_inc(weights_loaded, 16)
            sp.dma_start(a_cols[:, 0:1], a_l).then_inc(weights_loaded, 16)
            sp.dma_start(a_cols[:, 1:2], a_r).then_inc(weights_loaded, 16)
            sp.dma_start(proj_w[:, 0:D], w0_t).then_inc(weights_loaded, 16)
            sp.dma_start(bias_row[:], bias).then_inc(weights_loaded, 16)
            sp.dma_start(w1_sb[:], w1_t).then_inc(weights_loaded, 16)
            sp.dma_start(x_sb[:], x_rows.rearrange("(b p) d -> p b d", p=P)).then_inc(x_loaded, 16)
            for k in range(AHEAD, LOADS):
                load(0, k)
            with sp.Fori(1, PANELS) as q:
                for k in range(LOADS):
                    load(q, k)

        @block.gpsimd
        def _(pool):
            def gather(source, width, half, done, late, early=CHUNKS):
                pool.sem_inc(pool_gate, 1)
                for c in range(CHUNKS):
                    pool.indirect_dma_start(
                        out=gathered[:, half, c, 0:width], out_offset=None, in_=source,
                        in_offset=bass.IndirectOffsetOnAxis(ap=idx[:, half, c:c + 1], axis=0))\
                        .then_inc(done if c < early else late, 16)

            pool.wait_ge(table_stored, 16)

            def turn(q, half, now):
                pool.wait_ge(idx_ready, q + 1)
                wait(pool, att_summed, q - 1)
                gather(table_rows, TAB, half, rows_gathered[half], None)
                for c in range(SHARE):
                    choose(nc.gpsimd, half, c, edge_data[:, half, c, ROW:ROW + 1], share_ready)

            pipeline(pool, turn, 1)
            pool.wait_ge(att_summed, PANELS)
            for half in range(2):
                pool.wait_ge(scaled_free[half], 16 + 16 * PANELS // 2)

            def turn(q, half, now):
                pool.wait_ge(idx2_ready, q + 1)
                wait(pool, agg_done, q - 1)
                gather(scaled_rows, D, half, rows2_gathered[half], rows2_late[half], EARLY)

            pipeline(pool, turn, 1)

        @block.tensor
        def _(pe):
            def pack(q, k):
                pe.wait_ge(adj_loaded[k], 16 * q + 16)
                if k == 0:
                    wait(pe, words_summed, TILES * q)
                values = ring[:, k, :].bitcast(BF16).rearrange("p (b n two) -> p b n two", b=LBLOCKS, two=2)
                for b in range(LBLOCKS):
                    w = (k * LBLOCKS + b) * BWORDS
                    for j in range(TILES):
                        ins = nc.tensor.matmul(ps_words[:, j, w:w + BWORDS],
                                               lhsT=values[:, b, j * P:(j + 1) * P, 1], rhs=pack_w[:],
                                               start=True, stop=True)
                ins.then_inc(words_packed, 1)

            pe.wait_ge(ones_ready, 1)
            pe.wait_ge(line_loaded, 16)
            for k in range(4):
                nc.tensor.matmul(proj_out[k][:, 0:PIECE], lhsT=ones_row[:], rhs=line_sb[:, k * PIECE:(k + 1) * PIECE],
                                 start=True, stop=True).then_inc(line_spread, 1)
            pe.wait_ge(set_up, 5)
            for k in range(AHEAD):
                pack(0, k)
            pe.wait_ge(heads_ready, 1 + 2 * HEADS)
            nc.tensor.matmul(ps_slot[:, 0:2 * HEADS], lhsT=w0_sb[:], rhs=a_heads[:], start=True,
                             stop=True).then_inc(score_w_done, 1)
            nc.tensor.matmul(ps_edge[:, 0:D], lhsT=ones_row[:], rhs=bias_row[:], start=True,
                             stop=True).then_inc(bias_done, 1)
            pe.wait_ge(proj_w_ready, 1)
            pe.wait_ge(bias_saved, 1)
            pe.wait_ge(line_saved, 4)
            pe.wait_ge(x_loaded, 16)
            for g in range(BLOCKS // TILES + 1):
                if g < BLOCKS // TILES:
                    wait(pe, x_t_saved, g - 1)
                    for j in range(TILES):
                        ins = nc.tensor.matmul(turn_out[g % 2][:, j * P:(j + 1) * P], lhsT=x_sb[:, TILES * g + j, :],
                                               rhs=cst[:, C_IDENT:C_BEFORE], start=True, stop=True)
                    ins.then_inc(x_turned, 1)
                if g > 0:
                    pe.wait_ge(x_t_saved, g)
                    for t in range(TILES * (g - 1), TILES * g):
                        wait(pe, proj_saved, t - 3)
                        nc.tensor.matmul(proj_out[t % 4][:, 0:TAB], lhsT=x_t[:, t * P:(t + 1) * P], rhs=proj_w[:],
                                         start=True, stop=True).then_inc(proj_done, 1)
            pe.wait_ge(proj_saved, BLOCKS)

            def keep_warm(n):
                for _ in range(n):
                    nc.tensor.matmul(ps_words[:, 0:2, :].rearrange("p j w -> p (j w)"), lhsT=ones_w[:],
                                     rhs=row_data[:].rearrange("p t s -> p (t s)")[:, 0:BANK], start=True,
                                     stop=True)

            def slots(q, half):
                pe.wait_ge(select_ready, (CHUNKS - SHARE) * (q + 1))
                pe.wait_ge(share_ready, SHARE * (q + 1))
                pe.wait_ge(by_slot_ready, q + 1)
                for j in range(TILES):
                    for c in range(*WINDOW[j]):
                        ins = nc.tensor.matmul(slot_out[:, j, :], lhsT=select_cols(half, c, j),
                                               rhs=by_slot[:, c, :, :].rearrange("p s h -> p (s h)"),
                                               start=(c == WINDOW[j][0]), stop=(c == WINDOW[j][1] - 1))
                ins.then_inc(slots_done, 1)

            def firsts(q):
                pe.wait_ge(counted, q + 1)
                nc.tensor.matmul(ps_first[:, 0:TILES], lhsT=before_w[:], rhs=degree_w[:, tiles(q)], start=True,
                                 stop=True)
                for s in range(1, TILES):
                    ins = nc.tensor.matmul(ps_first[:, s:TILES], lhsT=ones_w[:],
                                           rhs=degree_w[:, bass.ds(TILES * q, TILES - s)], start=False,
                                           stop=True, skip_group_check=True)
                ins.then_inc(first_done, 1)

            def select_cols(half, c, j):
                k = j - TILES_OF[c][0]
                return select[:, half, c, k * P:(k + 1) * P]

            def spread_cols(half, c, j):
                return spread[:, half, j, (c - WINDOW[j][0]) * P:(c - WINDOW[j][0] + 1) * P]

            def hand_out(q, half):
                pe.wait_ge(spread_ready, TILES * q + TILES)
                wait(pe, edges_saved, q)
                for c in range(CHUNKS):
                    for j in TILES_OF[c]:
                        rows = spread_cols(half, c, j)
                        t = one(TILES * q + j)
                        nc.tensor.matmul(edge_out[:, c, :], lhsT=rows, rhs=row_data[:, t, 0:TAKEN],
                                         start=(j == TILES_OF[c][0]), stop=True, skip_group_check=True)
                        nc.tensor.matmul(edge_out[:, c, :], lhsT=rows, rhs=row_data[:, t, TAKEN:2 * TAKEN],
                                         start=False, stop=True, skip_group_check=True)
                        ins = nc.tensor.matmul(edge_out[:, c, LEFT:TAKEN], lhsT=rows,
                                               rhs=row_data[:, t, 2 * TAKEN:PARTS], start=False, stop=True,
                                               skip_group_check=True)
                ins.then_inc(edges_spread, 1)

            def shifts(q, half):
                pe.wait_ge(shift_ready, q + 1)
                for c in range(CHUNKS):
                    for j in TILES_OF[c]:
                        for k in range(2):
                            ins = nc.tensor.matmul(shift_out[:, c, :], lhsT=spread_cols(half, c, j),
                                                   rhs=shift_parts[:, j, k * HEADS:(k + 1) * HEADS],
                                                   start=(j == TILES_OF[c][0] and k == 0),
                                                   stop=(j == TILES_OF[c][-1] and k == 1))
                ins.then_inc(shift_spread, 1)

            def add_up(q, half):
                for j in range(TILES):
                    pe.wait_ge(weighted, CHUNKS // BATCH * q + (WINDOW[j][1] - 1) // BATCH + 1)
                    for c in range(*WINDOW[j]):
                        ins = nc.tensor.matmul(att_out[:, j // 2, j % 2, :], lhsT=select_cols(half, c, j),
                                               rhs=gathered[:, half, c, 0:D + HEADS],
                                               start=(c == WINDOW[j][0]), stop=(c == WINDOW[j][1] - 1))
                ins.then_inc(att_summed, 1)

            def turn(q, half, now):
                past = 1 - half

                def some(loads):
                    if 0 in now:
                        for k in loads:
                            if not (isinstance(q, int) and q == 0 and k < AHEAD):
                                pack(q, k)

                last = isinstance(q, int) and q > PANELS
                if 3 in now:
                    if last:
                        pe.wait_ge(words_summed, TILES * PANELS)
                    slots(q - 3, past)
                    if last:
                        keep_warm(14)
                some(range(0, 4))
                if 1 in now:
                    firsts(q - 1)
                if 3 in now:
                    shifts(q - 3, past)
                    if last:
                        keep_warm(4)
                some(range(4, 6))
                if 1 in now:
                    hand_out(q - 1, past)
                some(range(6, LOADS))
                if 3 in now:
                    add_up(q - 3, past)

            pipeline(pe, turn, 4)
            pe.wait_ge(bad_ready, 1)
            nc.tensor.matmul(ps_first[0:1, 0:1], lhsT=bad_row[:], rhs=cst[:, C_ROWS:C_ROWS + 1], start=True,
                             stop=True).then_inc(bad_summed, 1)

            def turn(q, half, now):
                out_cols = agg_out[half]
                pe.wait_ge(now_ready, TILES * q + TILES)
                wait(pe, agg_saved, q - 1)
                for j in range(TILES):
                    nc.tensor.matmul(out_cols[:, j * P:(j + 1) * P], lhsT=scaled[:, half, j, :], rhs=two_ident[:],
                                     start=(j == 0), stop=True, skip_group_check=True)
                pe.wait_ge(select2_ready, CHUNKS * q + CHUNKS)
                keep_warm(8)
                pe.wait_ge(rows2_gathered[half], 8 * EARLY * (q - half) + 16 * EARLY)
                for c in range(CHUNKS):
                    if c == EARLY:
                        pe.wait_ge(rows2_late[half], 8 * (CHUNKS - EARLY) * (q - half + 2))
                    cols = slice(TILES_OF[c][0] * P, (TILES_OF[c][-1] + 1) * P)
                    ins = nc.tensor.matmul(out_cols[:, cols], lhsT=gathered[:, half, c, 0:D],
                                           rhs=select[:, half, c, 0:len(TILES_OF[c]) * P], start=False, stop=True,
                                           skip_group_check=True)
                ins.then_inc(agg_done, 1)
                pe.wait_ge(agg_saved, q + 1)
                wait(pe, lin_taken, TILES * q)
                for j in range(TILES):
                    ins = nc.tensor.matmul(lin_out[:, j * D:(j + 1) * D], lhsT=agg_cols[:, j * P:(j + 1) * P],
                                           rhs=w1_sb[:], start=True, stop=True)
                ins.then_inc(lin_done, 1)

            pipeline(pe, turn, 1)

        @block.scalar
        def _(act):
            nc.scalar.preload_act_table_set("natural_log_exp_and_others")
            for k in range(4):
                act.wait_ge(line_spread, k + 1)
                nc.scalar.activation(cst[:, C_ROWS + k * PIECE:C_ROWS + (k + 1) * PIECE], proj_out[k][:, 0:PIECE],
                                     ACT.Copy).then_inc(line_saved, 1)
            for t in range(BLOCKS):
                act.wait_ge(proj_done, t + 1)
                nc.scalar.activation(table[:, t, :], proj_out[t % 4][:, 0:TAB], ACT.Copy).then_inc(proj_saved, 1)
            act.wait_ge(proj_saved, BLOCKS)
            act.dma_start(table_rows.rearrange("(b p) d -> p b d", p=P), table[:]).then_inc(table_stored, 16)
            act.wait_ge(line_saved, 4)
            act.wait_ge(set_up, 6)

            def words(q):
                act.wait_ge(words_packed, LOADS * q + LOADS)
                wait(act, words_taken, q)
                for j in range(TILES):
                    nc.scalar.activation(words_sb[:, j, :], ps_words[:, j, :], ACT.Copy,
                                         accum_out=packed_sum[:, one(TILES * q + j)]).then_inc(words_summed, 1)

            def distances(q, js):
                act.wait_ge(middle_ready, q + 1)
                wait(act, spread_ready, TILES * q)
                for j in js:
                    lo, hi = WINDOW[j]
                    nc.scalar.activation(distance[:, j, 0:(hi - lo) * P], cst[:, C_EDGES + lo * P:C_EDGES + hi * P],
                                         ACT.Abs, bias=off_middle[:, j:j + 1]).then_inc(distance_ready, 1)

            def root_degree(q):
                nc.scalar.activation(log_deg[:], degree[:, tiles(q)], ACT.Ln, bias=eps[:, 1:2]).then_inc(act_deg, 1)
                act.wait_ge(act_deg, q + 1)
                nc.scalar.activation(dis[:, tiles(q)], log_deg[:], ACT.Exp, scale=-0.5).then_inc(dis_done, 1)

            def turn(q, half, now):
                past = 1 - half
                if 0 in now:
                    words(q)
                if 4 in now:
                    p = q - 4
                    act.wait_ge(scaled_free[half], 8 * (p - half) + 16)
                    act.wait_ge(mean_ready, p + 1)
                    for j in range(TILES):
                        nc.scalar.activation(scaled[:, half, j, :], att[:, half, j, :], ACT.Identity,
                                             scale=rstd_dis[:, j:j + 1], bias=off_mean_dis[:, j:j + 1])\
                            .then_inc(scaled_ready, 1)
                    act.wait_ge(scaled_ready, TILES * p + TILES)
                    act.dma_start(scaled_rows.rearrange("(b p) d -> p b d", p=P)[:, tiles(p), :],
                                  scaled[:, half, :, :]).then_inc(scaled_free[half], 16)
                    for j in range(TILES):
                        nc.scalar.activation(hidden[:, one(TILES * p + j), :], att[:, half, j:j + 1, :], ACT.Identity,
                                             scale=rstd[:, j:j + 1], bias=off_mean[:, j:j + 1])\
                            .then_inc(hidden_ready, 1)
                if 3 in now:
                    p = q - 3
                    act.wait_ge(att_ready, p + 1)
                    nc.scalar.activation(att_exp[:], att[:, past, :, :], ACT.Exp).then_inc(att_exp_done, 1)
                    act.wait_ge(moments_ready, TILES * p + TILES)
                    nc.scalar.activation(log_var[:], moments[:, :, 1], ACT.Ln, bias=eps[:, 0:1]).then_inc(act_stat, 1)
                    act.wait_ge(act_stat, p + 1)
                    nc.scalar.activation(rstd[:], log_var[:], ACT.Exp, scale=-0.5).then_inc(rstd_done, 1)
                if 2 in now:
                    act.wait_ge(self_ready, q - 1)
                    nc.scalar.activation(self_prob[:, half, :, :], row_max[:, half, :, :], ACT.Exp)\
                        .then_inc(self_exp, 1)
                if 0 in now:
                    distances(q, [0])
                if 2 in now:
                    act.wait_ge(score_ready, q - 1)
                    nc.scalar.activation(edge_p[:], edge_s[:, 2, :, :], ACT.Exp).then_inc(score_exp, 1)
                if 0 in now:
                    distances(q, range(1, TILES))
                    root_degree(q)
                if 0 in now:
                    act.wait_ge(edges_spread, q + 1)
                    wait(act, share_ready, SHARE * (q - 1))
                    nc.scalar.activation(edge_data[:, half, :, :], edge_out, ACT.Copy).then_inc(edges_saved, 1)

            for half in range(2):
                act.sem_inc(scaled_free[half], 16)
            pipeline(act, turn, 5)
            for half in range(2):
                act.wait_ge(scaled_free[half], 16 + 16 * PANELS // 2)

            def turn(q, half, now):
                past = 1 - half
                if 0 in now:
                    wait(act, agg_done, q - 1)
                    for j in range(TILES):
                        nc.scalar.activation(scaled[:, half, j:j + 1, :], hidden[:, one(TILES * q + j), :], ACT.Copy,
                                             scale=dis[:, one(TILES * q + j)]).then_inc(now_ready, 1)
                if 2 in now:
                    p = q - 2
                    act.wait_ge(moments2_ready, TILES * p + TILES)
                    nc.scalar.activation(log_var[:], moments[:, :, 1], ACT.Ln, bias=eps[:, 0:1]).then_inc(act_stat2, 1)
                    act.wait_ge(act_stat2, p + 1)
                    nc.scalar.activation(rstd[:], log_var[:], ACT.Exp, scale=-0.5).then_inc(rstd2_done, 1)
                    act.wait_ge(rstd2_done, p + 1)
                    act.wait_ge(mean2_ready, p + 1)
                    wait(act, result_stored[half], 8 * (p - half))
                    for j in range(TILES):
                        nc.scalar.activation(result[:, half, j, :], att[:, half, j, :], ACT.Identity,
                                             scale=rstd[:, j:j + 1], bias=off_mean[:, j:j + 1])\
                            .then_inc(result_ready, 1)
                    act.wait_ge(result_ready, TILES * p + TILES)
                    act.dma_start(out.rearrange("(b p) d -> p b d", p=P)[:, tiles(p), :],
                                  result[:, half, :, :]).then_inc(result_stored[half], 16)
                if 1 in now:
                    act.wait_ge(agg_done, q)
                    wait(act, lin_done, q - 1)
                    nc.scalar.activation(agg_cols[:], agg_out[past], ACT.Copy).then_inc(agg_saved, 1)

            pipeline(act, turn, 3)
            for half in range(2):
                act.wait_ge(result_stored[half], 16 * PANELS // 2)

        @block.vector
        def _(dve):
            def gated():
                dve.sem_inc(vec_gate, 1)

            nc.vector.memset(ones_row[:], 1.0).then_inc(ones_ready, 1)
            nc.vector.memset(a_heads[:], 0.0).then_inc(heads_ready, 1)
            nc.vector.memset(ones_w[:], 1.0).then_inc(set_up, 1)
            nc.vector.memset(eps[:, 0:1], EPS).then_inc(set_up, 1)
            nc.vector.memset(eps[:, 1:2], 2.0).then_inc(set_up, 1)
            dve.wait_ge(consts_loaded, 16)
            nc.vector.tensor_copy(pack_w[:], cst[:, C_PACK:C_PLACE]).then_inc(set_up, 1)
            nc.vector.tensor_copy(before_w[:], cst[:, C_BEFORE:C_PACK]).then_inc(set_up, 1)
            nc.vector.tensor_scalar(two_ident[:], cst[:, C_IDENT:C_BEFORE], 2.0, None, ALU.mult).then_inc(set_up, 1)
            dve.wait_ge(weights_loaded, 16 * 6)
            dve.wait_ge(heads_ready, 1)
            for h in range(HEADS):
                for s in range(2):
                    nc.vector.tensor_copy(a_heads[h * DK:(h + 1) * DK, s * HEADS + h:s * HEADS + h + 1],
                                          a_cols[h * DK:(h + 1) * DK, s:s + 1]).then_inc(heads_ready, 1)
            dve.wait_ge(score_w_done, 1)
            nc.vector.tensor_copy(proj_w[:, D:TAB], ps_slot[:, 0:2 * HEADS]).then_inc(proj_w_ready, 1)
            dve.wait_ge(bias_done, 1)
            nc.vector.tensor_copy(bias_sb[:], ps_edge[:, 0:D]).then_inc(bias_saved, 1)
            for g in range(BLOCKS // TILES):
                dve.wait_ge(x_turned, g + 1)
                nc.vector.tensor_copy(x_t[:, g * ROWS:(g + 1) * ROWS], turn_out[g % 2][:]).then_inc(x_t_saved, 1)
            dve.wait_ge(proj_saved, BLOCKS)
            dve.wait_ge(line_saved, 4)
            mark, settle, link, taken = counter(dve, vec_setup, 0, 0)
            left, right = table[:, :, D:D + HEADS], table[:, :, D + HEADS:TAB]
            part = [row_data[:, :, s:s + HEADS] for s in (LEFT, TAKEN + LEFT, 2 * TAKEN)]
            number = [row_data[:, :, s] for s in (ROW, TAKEN + ROW)]
            link(nc.vector.tensor_copy(number[0], cst[:, C_ROW:C_ROW + BLOCKS]),
                 nc.vector.tensor_copy(number[1], cst[:, C_ROW + BLOCKS:C_BASE]),
                 nc.vector.tensor_copy(part[0], left),
                 nc.vector.tensor_tensor(self_score[:], left, right, ALU.add))
            link(nc.vector.scalar_tensor_tensor(out=self_score[:], in0=self_score[:], scalar=SLOPE, in1=self_score[:],
                                                op0=ALU.mult, op1=ALU.max),
                 nc.vector.tensor_tensor(left_rest[:], left, part[0], ALU.subtract))
            link(nc.vector.tensor_copy(part[1], left_rest[:]))
            link(nc.vector.tensor_tensor(left_rest[:], left_rest[:], part[1], ALU.subtract))
            link(nc.vector.tensor_copy(part[2], left_rest[:]))

            FIND, PLACE, INDEX, SLOT = 7 * TILES + 5 * LEVELS + 10, 4, 7, 3
            MAX, WEIGH, ATT, NORM = 7, 1, 6, TILES + 4

            def find(q, half):
                mark, settle, link, taken = counter(dve, vec_find, FIND, q)
                sides = [(j, s, words_sb[:, j, s * WORDS // 2:(s + 1) * WORDS // 2]) for j in range(TILES)
                         for s in range(2)]
                dve.wait_ge(words_summed, TILES * q + TILES)
                gated()
                mark(*(nc.vector.max(top[:, 0, j, 8 * s:8 * s + 8], w) for j, s, w in sides))
                yield
                settle()
                gated()
                mark(*(nc.vector.max_index(where[:, j, 8 * s:8 * s + 8], top[:, 0, j, 8 * s:8 * s + 8], w)
                       for j, s, w in sides))
                exponent, power = bit[:, 0, :, :], bit[:, 1, :, :]
                for level in range(LEVELS):
                    v = top[:, level, :, :]
                    mark(nc.vector.tensor_scalar(exponent, v.bitcast(I32), 23, None, ALU.logical_shift_right),
                         nc.vector.tensor_scalar(power, v.bitcast(I32), 0xFF << 23, None, ALU.bitwise_and))
                    if level == 0:
                        yield
                        settle()
                        dve.sem_inc(words_taken, 1)
                        mark(*(nc.vector.tensor_scalar(word_key[:, :, 8 * s:8 * s + 8], where[:, :, 8 * s:8 * s + 8],
                                                       float(BITS), float(s * N // 2 + 1 - 127), ALU.mult, ALU.add)
                               for s in range(2)))
                    else:
                        mark(nc.vector.scalar_tensor_tensor(out=all_keys[:, :, level - 1, :],
                                                            in0=top[:, level - 1, :, :], scalar=0.0,
                                                            in1=key_tmp[:, level - 1, :, :], op0=ALU.is_gt,
                                                            op1=ALU.mult))
                    yield
                    settle()
                    mark(nc.vector.tensor_tensor(key_tmp[:, level, :, :], exponent, word_key[:], ALU.add),
                         nc.vector.tensor_tensor(top[:, level + 1, :, :], v, power.bitcast(F32), ALU.subtract))
                    yield
                    settle()
                mark(nc.vector.scalar_tensor_tensor(out=all_keys[:, :, LEVELS - 1, :], in0=v, scalar=0.0,
                                                    in1=key_tmp[:, LEVELS - 1, :, :], op0=ALU.is_gt, op1=ALU.mult),
                     nc.vector.tensor_tensor(key_tmp[:, LEVELS, :, :], top[:, 0, :, :], top[:, LEVELS, :, :],
                                             ALU.subtract))
                yield
                settle()
                mark(nc.vector.tensor_reduce(found[:, tiles(q)], key_tmp[:, LEVELS, :, :], AX_X, ALU.add))
                every = [all_keys[:, j, :, :].rearrange("p l s -> p (l s)") for j in range(TILES)]
                mark(*(nc.vector.max(keys[:, j, 0:8], every[j]) for j in range(TILES)))
                yield
                settle()
                gated()
                mark(*(nc.vector.match_replace(rest_keys[:, j, :], keys[:, j, 0:8], every[j], 0.0)
                       for j in range(TILES)))
                yield
                settle()
                gated()
                mark(*(nc.vector.max(keys[:, j, 8:16], rest_keys[:, j, :]) for j in range(TILES)))
                yield
                settle()
                wait(dve, vec_max, MAX * (q - 2) + 1)
                mark(nc.vector.tensor_scalar(key_tmp[:, 0, :, :], keys[:], 0.0, None, ALU.is_gt),
                     nc.vector.tensor_scalar(no_key[:, half, :, :], keys[:], 0.0, -FAR, ALU.is_le, ALU.mult),
                     nc.vector.tensor_copy(row_data[:, tiles(q), KEY:KEY + SLOTS], keys[:]),
                     nc.vector.tensor_copy(last_key[:, tiles(q)], keys[:, :, SLOTS - 1]))
                yield
                settle()
                mark(nc.vector.tensor_reduce(degree[:, tiles(q)], key_tmp[:, 0, :, :], AX_X, ALU.add),
                     nc.vector.tensor_tensor(row_data[:, tiles(q), TAKEN + KEY:TAKEN + KEY + SLOTS], keys[:],
                                             row_data[:, tiles(q), KEY:KEY + SLOTS], ALU.subtract))
                yield
                settle()
                nc.vector.tensor_copy(degree_w[:, tiles(q)], degree[:, tiles(q)]).then_inc(counted, 1)
                assert taken() == FIND, ("FIND", taken())

            def place(q, half):
                mark, settle, link, taken = counter(dve, vec_place, PLACE, q)
                dve.wait_ge(first_done, q + 1)
                a = ps_first[:, 0:TILES]
                nc.vector.scalar_tensor_tensor(out=off_middle[:], in0=a, scalar=-2.0, in1=degree[:, tiles(q)],
                                               op0=ALU.mult, op1=ALU.subtract).then_inc(middle_ready, 1)
                mark(nc.vector.tensor_copy(row_data[:, tiles(q), FIRST], a),
                     nc.vector.tensor_copy(first[:, tiles(q)], a))
                yield
                settle()
                mark(nc.vector.tensor_tensor(row_data[:, tiles(q), TAKEN + FIRST], first[:, tiles(q)],
                                             row_data[:, tiles(q), FIRST], ALU.subtract),
                     nc.vector.tensor_tensor(behind[:, tiles(q)], first[:, tiles(q)], degree[:, tiles(q)], ALU.add))
                wait(dve, shift_spread, q - 1)
                for j in range(TILES):
                    yield
                    dve.wait_ge(distance_ready, TILES * q + j + 1)
                    if j == 0:
                        settle()
                    wide = (WINDOW[j][1] - WINDOW[j][0]) * P
                    nc.vector.tensor_scalar(spread[:, half, j, 0:wide], distance[:, j, 0:wide],
                                            degree[:, one(TILES * q + j)], None, ALU.is_lt).then_inc(spread_ready, 1)
                assert taken() == PLACE, ("PLACE", taken())

            def index(q, half):
                mark, settle, link, taken = counter(dve, vec_index, INDEX, q)
                data = edge_data[:, half, :, :]
                wide = [P, CHUNKS, SLOTS]
                dve.wait_ge(edges_saved, q + 1)
                mark(nc.vector.tensor_tensor(edge_pos[:], cst[:, C_PLACE:C_SLOT], data[:, :, FIRST], ALU.subtract))
                yield
                settle()
                mark(nc.vector.tensor_tensor(edge_mask[:, half, :, :],
                                             cst[:, C_SLOT:C_ROW].unsqueeze(1).to_broadcast(wide),
                                             edge_pos[:].unsqueeze(2).to_broadcast(wide), ALU.is_equal))
                yield
                settle()
                mark(nc.vector.tensor_tensor(edge_keys[:], data[:, :, KEY:KEY + SLOTS], edge_mask[:, half, :, :],
                                             ALU.mult))
                yield
                settle()
                mark(nc.vector.tensor_reduce(edge_key[:, half, :], edge_keys[:], AX_X, ALU.add))
                yield
                settle()
                mark(nc.vector.tensor_scalar(edge_pos[:], edge_key[:, half, :], 1.0, float(N), ALU.max, ALU.min))
                yield
                settle()
                nc.vector.tensor_scalar(idx[:, half, :], edge_pos[:], -1.0, None, ALU.add).then_inc(idx_ready, 1)
                mark(nc.vector.tensor_scalar(all_idx[:, one(q), :], edge_pos[:].unsqueeze(1), -1.0, None, ALU.add),
                     nc.vector.tensor_copy(all_row[:, one(q), :], data[:, :, ROW].unsqueeze(1)))
                assert taken() == INDEX, ("INDEX", taken())

            def slot(q, half):
                mark, settle, link, taken = counter(dve, vec_slot, SLOT, q)
                data = edge_data[:, half, :, :]
                for c in range(SHARE, CHUNKS):
                    choose(nc.vector, half, c, data[:, c, ROW:ROW + 1], select_ready)
                dve.wait_ge(rows_gathered[half], 8 * CHUNKS * (q - half) + 16 * CHUNKS)
                wide = [P, CHUNKS, SLOTS, HEADS]
                r = gathered[:, half, :, D + HEADS:TAB]
                nc.vector.tensor_tensor(by_slot[:], edge_mask[:, half, :, :].unsqueeze(3).to_broadcast(wide),
                                        r.unsqueeze(2).to_broadcast(wide), ALU.mult).then_inc(by_slot_ready, 1)
                mark(nc.vector.tensor_tensor(edge_s[:, 0, :, :], data[:, :, LEFT:TAKEN], r, ALU.add),
                     nc.vector.scalar_tensor_tensor(out=other[:], in0=data[:, :, ROW],
                                                    scalar=cst[:, bass.ds(q + C_BASE, 1)],
                                                    in1=edge_key[:, half, :], op0=ALU.add, op1=ALU.not_equal))
                yield
                settle()
                mark(nc.vector.scalar_tensor_tensor(out=edge_s[:, 1, :, :], in0=edge_s[:, 0, :, :], scalar=SLOPE,
                                                    in1=edge_s[:, 0, :, :], op0=ALU.mult, op1=ALU.max))
                assert taken() == SLOT, ("SLOT", taken())

            def greatest(q, half):
                mark, settle, link, taken = counter(dve, vec_max, MAX, q)
                m = row_max[:, half, :, :]
                dve.wait_ge(slots_done, q + 1)
                mark(nc.vector.tensor_tensor(slot_r[:], slot_out.rearrange("p j (s h) -> p j s h", h=HEADS),
                                             no_key[:, half, :, :].unsqueeze(3).to_broadcast([P, TILES, SLOTS, HEADS]),
                                             ALU.add))
                yield
                settle()
                mark(nc.vector.tensor_reduce(m, slot_r[:].rearrange("p j s h -> p j h s"), AX_X, ALU.max))
                yield
                settle()
                mark(nc.vector.tensor_tensor(m, m, table[:, tiles(q), D + HEADS:TAB], ALU.max))
                yield
                settle()
                mark(nc.vector.tensor_tensor(m, m, table[:, tiles(q), D:D + HEADS], ALU.add))
                yield
                settle()
                mark(nc.vector.scalar_tensor_tensor(out=m, in0=m, scalar=SLOPE, in1=m, op0=ALU.mult, op1=ALU.max))
                yield
                settle()
                mark(nc.vector.tensor_copy(shift_parts[:, :, 0:HEADS], m))
                yield
                settle()
                nc.vector.tensor_tensor(shift_parts[:, :, HEADS:2 * HEADS], m, shift_parts[:, :, 0:HEADS],
                                        ALU.subtract).then_inc(shift_ready, 1)
                yield
                dve.wait_ge(shift_ready, q + 1)
                mark(nc.vector.tensor_tensor(shift[:], shift_parts[:, :, 0:HEADS], shift_parts[:, :, HEADS:2 * HEADS],
                                             ALU.add))
                yield
                settle()
                nc.vector.tensor_tensor(m, self_score[:, tiles(q), :], shift[:], ALU.subtract).then_inc(self_ready, 1)
                assert taken() == MAX, ("MAX", taken())

            def weigh(q, half):
                mark, settle, link, taken = counter(dve, vec_weight, WEIGH, q)
                dve.wait_ge(shift_spread, q + 1)
                nc.vector.tensor_tensor(edge_s[:, 2, :, :], edge_s[:, 1, :, :], shift_out, ALU.subtract)\
                    .then_inc(score_ready, 1)
                yield
                dve.wait_ge(score_exp, q + 1)
                mark(nc.vector.scalar_tensor_tensor(out=gathered[:, half, :, D:D + HEADS], in0=edge_p[:], scalar=FAR,
                                                    in1=other[:].unsqueeze(2).to_broadcast([P, CHUNKS, HEADS]),
                                                    op0=ALU.min, op1=ALU.mult))
                yield
                settle()
                rows = gathered[:, half, :, 0:D].rearrange("p c (h d) -> p c h d", h=HEADS)
                for c in range(0, CHUNKS, BATCH):
                    nc.vector.tensor_tensor(
                        rows[:, c:c + BATCH, :, :], rows[:, c:c + BATCH, :, :],
                        gathered[:, half, c:c + BATCH, D:D + HEADS].unsqueeze(3).to_broadcast([P, BATCH, HEADS, DK]),
                        ALU.mult).then_inc(weighted, 1)
                    yield
                assert taken() == WEIGH, ("WEIGH", taken())

            def attend(q, half):
                mark, settle, link, taken = counter(dve, vec_att, ATT, q)
                wide = [P, TILES, HEADS, DK]
                a = att[:, half, :, :]
                heads = a.rearrange("p j (h d) -> p j h d", h=HEADS)
                dve.wait_ge(self_exp, q + 1)
                mark(nc.vector.tensor_tensor(heads,
                                             table[:, tiles(q), 0:D].rearrange("p j (h d) -> p j h d", h=HEADS),
                                             self_prob[:, half, :, :].unsqueeze(3).to_broadcast(wide), ALU.mult))
                yield
                dve.wait_ge(att_summed, q + 1)
                for k in range(2):
                    mark(nc.vector.tensor_tensor(quotient[:, 0, 2 * k:2 * k + 2, :],
                                                 self_prob[:, half, 2 * k:2 * k + 2, :],
                                                 att_out[:, k, :, D:D + HEADS], ALU.add))
                settle()
                for k in range(2):
                    mark(nc.vector.tensor_tensor(a[:, 2 * k:2 * k + 2, :], a[:, 2 * k:2 * k + 2, :],
                                                 att_out[:, k, :, 0:D], ALU.add))
                mark(nc.vector.reciprocal(quotient[:, 1, :, :], quotient[:, 0, :, :]))
                yield
                settle()
                nc.vector.tensor_tensor(heads, heads, quotient[:, 1, :, :].unsqueeze(3).to_broadcast(wide), ALU.mult)\
                    .then_inc(att_ready, 1)
                assert taken() == ATT, ("ATT", taken())

            def moment(q, half):
                mark, settle, link, taken = counter(dve, vec_norm, NORM, q)
                a = att[:, half, :, :]
                dve.wait_ge(x_loaded, 16)
                dve.wait_ge(att_exp_done, q + 1)
                mark(nc.vector.scalar_tensor_tensor(out=att_exp[:], in0=att_exp[:], scalar=1.0,
                                                    in1=x_sb[:, tiles(q), :], op0=ALU.min, op1=ALU.add))
                yield
                settle()
                mark(nc.vector.scalar_tensor_tensor(out=a, in0=a, scalar=0.0, in1=att_exp[:], op0=ALU.max,
                                                    op1=ALU.add))
                yield
                settle()
                mark(*(nc.vector.bn_stats(stats[:, j, :], a[:, j, :]) for j in range(TILES)))
                yield
                settle()
                gated()
                for j in range(TILES):
                    nc.vector.bn_aggr(moments[:, j, :], stats[:, j, :]).then_inc(moments_ready, 1)
                yield
                dve.wait_ge(rstd_done, q + 1)
                mark(nc.vector.scalar_tensor_tensor(out=off_mean[:], in0=moments[:, :, 0], scalar=-1.0, in1=rstd[:],
                                                    op0=ALU.mult, op1=ALU.mult),
                     nc.vector.tensor_tensor(rstd_dis[:], rstd[:], dis[:, tiles(q)], ALU.mult))
                yield
                settle()
                nc.vector.tensor_tensor(off_mean_dis[:], off_mean[:], dis[:, tiles(q)], ALU.mult)\
                    .then_inc(mean_ready, 1)
                assert taken() == NORM, ("NORM", taken())

            def turn(q, half, now):
                past = 1 - half
                alternate(*([find(q, half)] if 0 in now else []),
                          *([later(1, in_turn(attend(q - 3, past), later(1, moment(q - 3, past))))]
                            if 3 in now else []),
                          *([later(6, greatest(q - 2, half))] if 2 in now else []))
                alternate(*([place(q, half)] if 0 in now else []),
                          *([weigh(q - 2, half)] if 2 in now else []))
                alternate(*([slot(q - 1, past)] if 1 in now else []))
                alternate(*([index(q, half)] if 0 in now else []))
            pipeline(dve, turn, 4)

            mark, settle, link, taken = counter(dve, vec_flag, 0, 0)
            link(nc.vector.tensor_tensor(bad[:, 0, :], found[:], packed_sum[:], ALU.not_equal),
                 nc.vector.tensor_scalar(bad[:, 1, :], last_key[:], 0.0, None, ALU.is_gt),
                 nc.vector.tensor_tensor(bad[:, 2, :], first[:], cst[:, C_LOW:C_HIGH], ALU.is_lt),
                 nc.vector.tensor_tensor(bad[:, 3, :], behind[:], cst[:, C_HIGH:C_ROWS], ALU.is_gt))
            nc.vector.tensor_reduce(bad_row[:], bad[:].rearrange("p k t -> p (k t)"), AX_X, ALU.add)\
                .then_inc(bad_ready, 1)
            dve.wait_ge(bad_summed, 1)
            nc.vector.tensor_copy(flag[:], ps_first[0:1, 0:1]).then_inc(flag_set, 1)

            TWO = TILES + 1

            def turn(q, half, now):
                if 0 in now:
                    wait(dve, rows2_gathered[half], 8 * EARLY * (q - half))
                    gated()
                    wait(dve, rows2_late[half], 8 * (CHUNKS - EARLY) * (q - half))
                    nc.vector.tensor_copy(idx[:, half:half + 1, :], all_idx[:, one(q), :]).then_inc(idx2_ready, 1)
                    wait(dve, agg_done, q - 1)
                    for c in range(CHUNKS):
                        choose(nc.vector, half, c, all_row[:, one(q), c:c + 1], select2_ready)
                if 2 in now:
                    p = q - 2
                    mark, settle, link, taken = counter(dve, vec_two, TWO, p)
                    a = att[:, half, :, :]
                    dve.wait_ge(lin_done, p + 1)
                    wait(dve, result_ready, TILES * (p - 1))
                    for j in range(TILES):
                        nc.vector.scalar_tensor_tensor(out=a[:, j:j + 1, :],
                                                       in0=lin_out[:, j * D:(j + 1) * D].unsqueeze(1),
                                                       scalar=dis[:, one(TILES * p + j)],
                                                       in1=bias_sb[:].unsqueeze(1),
                                                       op0=ALU.mult, op1=ALU.add).then_inc(lin_taken, 1)
                    dve.wait_ge(lin_taken, TILES * p + TILES)
                    link(nc.vector.scalar_tensor_tensor(out=a, in0=a, scalar=0.0, in1=hidden[:, tiles(p), :],
                                                        op0=ALU.max, op1=ALU.add))
                    link(*(nc.vector.bn_stats(stats[:, j, :], a[:, j, :]) for j in range(TILES)))
                    gated()
                    for j in range(TILES):
                        nc.vector.bn_aggr(moments[:, j, :], stats[:, j, :]).then_inc(moments2_ready, 1)
                    dve.wait_ge(rstd2_done, p + 1)
                    nc.vector.scalar_tensor_tensor(out=off_mean[:], in0=moments[:, :, 0], scalar=-1.0, in1=rstd[:],
                                                   op0=ALU.mult, op1=ALU.mult).then_inc(mean2_ready, 1)
                    assert taken() == TWO, ("TWO", taken())

            pipeline(dve, turn, 3)
            dve.wait_ge(flag_set, 1)


def general_path(nc, flag, x_rows, x_cols, adj, adj_cols, w0, w0_t, a_l, a_r, w1_t, bias, out):
    with ExitStack() as ctx:
        def sb(name, shape, dt=F32):
            return ctx.enter_context(nc.sbuf_tensor("g_" + name, shape, dt))

        def sem(name):
            return ctx.enter_context(nc.semaphore("g_" + name))

        ident = sb("ident", [P, P])
        two_ident = sb("two_ident", [P, P])
        ones = sb("ones", [P, P])
        half_neg = sb("half_neg", [P, 2 * TILES])
        x_sb = sb("x_sb", [P, BLOCKS, D])
        w0_sb = sb("w0_sb", [D, D])
        w1_sb = sb("w1_sb", [D, D])
        bias_row = sb("bias_row", [1, D])
        bias_sb = sb("bias_sb", [P, D])
        a_cols = sb("a_cols", [D, 2])
        a_heads = sb("a_heads", [D, 2 * HEADS])
        proj_w = sb("proj_w", [D, TAB])
        score_w = sb("score_w", [D, HEADS, P])
        table = sb("table", [P, BLOCKS, TAB])
        r_rows = sb("r_rows", [P, HEADS, N])
        adj_sb = sb("adj_sb", [P, N])
        pen = sb("pen", [P, N])
        scores = sb("scores", [P, 2, N])
        probs_t = sb("probs_t", [P, BLOCKS, P])
        hidden = sb("hidden", [P, BLOCKS, D])
        neg_max = sb("neg_max", [P, 4])
        denom = sb("denom", [P, BLOCKS, HEADS])
        degree = sb("degree", [P, BLOCKS])
        dis = sb("dis", [P, BLOCKS])
        work = sb("work", [P, 3, TILES, D])
        small = sb("small", [P, 8 * TILES])
        stats = sb("stats", [P, TILES, 6])
        moments = sb("moments", [P, TILES, 2])
        powers = sb("powers", [P, 2, 2 * TILES])
        x_t = probs_t[:].rearrange("p b n -> p (b n)")
        scaled = probs_t
        panel = r_rows[:].rearrange("p h n -> p (h n)").rearrange("p (b n) -> p b n", b=BLOCKS)
        panel_agg = adj_sb[:, 0:ROWS]

        ps = ctx.enter_context(nc.psum_tensor("g_ps", [P, 8, BANK], F32))

        loaded = sem("loaded")
        constants = sem("constants")
        a_ready = sem("a_ready")
        score_w_done = sem("score_w_done")
        proj_w_ready = sem("proj_w_ready")
        score_w_ready = sem("score_w_ready")
        bias_done = sem("bias_done")
        proj_done = sem("proj_done")
        proj_saved = sem("proj_saved")
        rbc_done = sem("rbc_done")
        rbc_saved = sem("rbc_saved")

        adj_loaded = sem("adj_loaded")
        adj_used = sem("adj_used")
        vec_att = sem("vec_att")
        scores_ready = sem("scores_ready")
        scores_free = sem("scores_free")
        probs_ready = sem("probs_ready")
        transposed = sem("transposed")
        transposed_saved = sem("transposed_saved")
        group_summed = sem("group_summed")
        sums_done = sem("sums_done")
        sums_saved = sem("sums_saved")

        vec_gate = sem("vec_gate")
        vec_one = sem("vec_one")
        elu_in = sem("elu_in")
        elu_exp = sem("elu_exp")
        pow_in = sem("pow_in")
        pow_out = sem("pow_out")

        panel_loaded = sem("panel_loaded")
        diag_added = sem("diag_added")
        panel_summed = sem("panel_summed")
        agg_saved = sem("agg_saved")
        lin_done = sem("lin_done")
        vec_two = sem("vec_two")
        pow2_in = sem("pow2_in")
        pow2_out = sem("pow2_out")
        out_ready = sem("out_ready")
        out_free = sem("out_free")
        scaled_ready = sem("scaled_ready")
        out_stored = sem("out_stored")

        block = ctx.enter_context(nc.Block())

        @block.sync
        def _(sp):
            with sp.If(sp.value_load(flag[0:1, 0:1]) != 0):
                sp.dma_start(x_t, x_cols).then_inc(loaded, 16)
                sp.dma_start(proj_w[:, 0:D], w0_t).then_inc(loaded, 16)
                sp.dma_start(w0_sb[:], w0).then_inc(loaded, 16)
                sp.dma_start(a_cols[:, 0:1], a_l).then_inc(loaded, 16)
                sp.dma_start(a_cols[:, 1:2], a_r).then_inc(loaded, 16)
                sp.dma_start(bias_row[:], bias).then_inc(loaded, 16)
                sp.dma_start(w1_sb[:], w1_t).then_inc(loaded, 16)
                sp.dma_start(x_sb[:], x_rows.rearrange("(b p) d -> p b d", p=P)).then_inc(loaded, 16)
                sp.dma_start(adj_sb[:], adj[0:P, :]).then_inc(adj_loaded, 16)
                with sp.Fori(1, BLOCKS) as t:
                    sp.wait_ge(adj_used, t)
                    sp.dma_start(adj_sb[:], adj[bass.ds(t * P, P), :]).then_inc(adj_loaded, 16)
                sp.wait_ge(transposed, BLOCKS * HEADS * 8)
                sp.dma_start(panel, adj_cols[0]).then_inc(panel_loaded, 16)
                with sp.Fori(1, PANELS) as q:
                    sp.wait_ge(panel_summed, q)
                    sp.dma_start(panel, adj_cols[q]).then_inc(panel_loaded, 16)
                sp.wait_ge(out_stored, 16 * PANELS)

        @block.gpsimd
        def _(pool):
            with pool.If(pool.value_load(flag[0:1, 0:1]) != 0):
                nc.gpsimd.memset(ones[:], 1.0).then_inc(constants, 1)
                nc.gpsimd.memset(half_neg[:], -0.5).then_inc(constants, 1)
                pool.wait_ge(constants, 2)
                nc.gpsimd.affine_select(out=ident[:], in_=ones[:], compare_op=ALU.is_equal, fill=0.0, base=0,
                                        pattern=[[-1, P]], channel_multiplier=1).then_inc(constants, 1)
                with pool.Fori(0, PANELS) as q:
                    pool.wait_ge(pow_in, 2 * q + 2)
                    nc.gpsimd.tensor_tensor(powers[:, 1, :], powers[:, 0, :], half_neg[:], ALU.pow).then_inc(pow_out, 1)
                with pool.Fori(0, PANELS) as q:
                    pool.wait_ge(pow2_in, q + 1)
                    nc.gpsimd.tensor_tensor(powers[:, 1, 0:TILES], powers[:, 0, 0:TILES], half_neg[:, 0:TILES],
                                            ALU.pow).then_inc(pow2_out, 1)

        @block.scalar
        def _(act):
            with act.If(act.value_load(flag[0:1, 0:1]) != 0):
                act.sem_inc(rbc_saved, 1)
                act.sem_inc(transposed_saved, 4)
                act.sem_inc(sums_saved, 1)
                act.sem_inc(out_free, 1)
                with act.Fori(0, BLOCKS // 4) as u:
                    for k in range(4):
                        act.wait_ge(proj_done, 4 * u + k + 1)
                        nc.scalar.activation(table[:, bass.ds(4 * u + k, 1), :], ps[:, k:k + 1, 0:TAB],
                                             ACT.Copy).then_inc(proj_saved, 1)
                for k in range(HEADS):
                    with act.Fori(0, N // BANK) as c:
                        act.wait_ge(rbc_done, k * (N // BANK) + c + 1)
                        nc.scalar.activation(r_rows[:, k, bass.ds(c * BANK, BANK)], ps[:, 7, :],
                                             ACT.Copy).then_inc(rbc_saved, 1)
                with act.Fori(0, BLOCKS) as t:
                    for h in range(HEADS):
                        act.wait_ge(scores_ready, HEADS * t + h + 1)
                        nc.scalar.activation(scores[:, h % 2, :], scores[:, h % 2, :], ACT.Exp,
                                             bias=neg_max[:, h:h + 1],
                                             accum_out=denom[:, bass.ds(t, 1), h:h + 1]).then_inc(probs_ready, 1)
                        for g in range(8):
                            act.wait_ge(transposed, (HEADS * t + h) * 8 + g + 1)
                            act.wait_ge(group_summed, (HEADS * t + h) * 8 + g + 1)
                            nc.scalar.activation(probs_t[:, 4 * g:4 * g + 4, :],
                                                 ps[:, g % 4, :].rearrange("p (b n) -> p b n", b=4),
                                                 ACT.Copy).then_inc(transposed_saved, 1)
                    act.wait_ge(sums_done, t + 1)
                    nc.scalar.activation(hidden[:, bass.ds(t, 1), :], ps[:, 4:5, 0:D], ACT.Copy).then_inc(sums_saved, 1)
                with act.Fori(0, PANELS) as q:
                    act.wait_ge(elu_in, q + 1)
                    nc.scalar.activation(work[:, 1, :, :], work[:, 0, :, :], ACT.Exp).then_inc(elu_exp, 1)
                with act.Fori(0, PANELS) as q:
                    act.wait_ge(panel_summed, q + 1)
                    nc.scalar.activation(panel_agg, ps[:, 5, 0:ROWS], ACT.Copy).then_inc(agg_saved, 1)
                    act.wait_ge(out_ready, TILES * q + TILES)
                    act.dma_start(out.rearrange("(b p) d -> p b d", p=P)[:, bass.ds(TILES * q, TILES), :],
                                  work[:, 2, :, :]).then_inc(out_stored, 16)
                    act.wait_ge(out_stored, 16 * q + 16)
                    act.sem_inc(out_free, 1)
                act.wait_ge(out_stored, 16 * PANELS)

        @block.vector
        def _(dve):
            with dve.If(dve.value_load(flag[0:1, 0:1]) != 0):
                nc.vector.memset(a_heads[:], 0.0).then_inc(a_ready, 1)
                dve.wait_ge(loaded, 16 * 8)
                dve.wait_ge(a_ready, 1)
                for h in range(HEADS):
                    for s in range(2):
                        nc.vector.tensor_copy(a_heads[h * DK:(h + 1) * DK, s * HEADS + h:s * HEADS + h + 1],
                                              a_cols[h * DK:(h + 1) * DK, s:s + 1]).then_inc(a_ready, 1)
                dve.wait_ge(score_w_done, 1)
                nc.vector.tensor_copy(proj_w[:, D:TAB], ps[:, 5, 0:2 * HEADS]).then_inc(proj_w_ready, 1)
                dve.wait_ge(constants, 3)
                dve.wait_ge(proj_w_ready, 1)
                for h in range(HEADS):
                    nc.vector.tensor_scalar(score_w[:, h, :], ones[:], proj_w[:, D + HEADS + h:D + HEADS + h + 1], None,
                                            ALU.mult).then_inc(score_w_ready, 1)
                nc.vector.tensor_scalar(two_ident[:], ident[:], 2.0, None, ALU.mult).then_inc(score_w_ready, 1)
                dve.wait_ge(bias_done, 1)
                nc.vector.tensor_copy(bias_sb[:], ps[:, 6, 0:D]).then_inc(score_w_ready, 1)
                dve.wait_ge(score_w_ready, HEADS + 2)
                dve.wait_ge(rbc_saved, HEADS * (N // BANK) + 1)
                dve.wait_ge(proj_saved, BLOCKS)

                PER = 3 + 3 * HEADS
                with dve.Fori(0, BLOCKS) as t:
                    mark, settle, link, taken = counter(dve, vec_att, PER, t)
                    dve.wait_ge(adj_loaded, 16 * t + 16)
                    diag = adj_sb[:, bass.ds(t * P, P)]
                    link(nc.vector.tensor_tensor(diag, diag, ident[:], ALU.add))
                    link(nc.vector.tensor_reduce(degree[:, bass.ds(t, 1)], adj_sb[:], AX_X, ALU.add),
                              nc.vector.tensor_scalar(pen[:], adj_sb[:], 0.0, -FAR, ALU.is_le, ALU.mult))
                    dve.sem_inc(adj_used, 1)
                    for h in range(HEADS):
                        s = scores[:, h % 2, :]
                        dve.wait_ge(scores_free, HEADS * t + h + 1)
                        link(nc.vector.tensor_scalar(s, r_rows[:, h, :], table[:, bass.ds(t, 1), D + h:D + h + 1],
                                                          None, ALU.add))
                        link(nc.vector.scalar_tensor_tensor(out=s, in0=s, scalar=SLOPE, in1=s, op0=ALU.mult,
                                                                 op1=ALU.max))
                        dve.sem_inc(vec_gate, 1)
                        link(nc.vector.tensor_tensor_reduce(out=s, in0=s, in1=pen[:], scale=1.0, scalar=-3.0e38,
                                                                 op0=ALU.add, op1=ALU.max, accum_out=small[:, h:h + 1]))
                        nc.vector.tensor_scalar(neg_max[:, h:h + 1], small[:, h:h + 1], -1.0, None,
                                                ALU.mult).then_inc(scores_ready, 1)
                    assert taken() == PER

                dve.wait_ge(sums_saved, BLOCKS + 1)
                dve.wait_ge(scores_ready, BLOCKS * HEADS)
                PER = 3 + 8 * TILES
                with dve.Fori(0, PANELS) as q:
                    mark, settle, link, taken = counter(dve, vec_one, PER, q)
                    att = work[:, 2, :, :]
                    for j in range(TILES):
                        one = bass.ds(TILES * q + j, 1)
                        r = small[:, j * HEADS:(j + 1) * HEADS]
                        link(nc.vector.reciprocal(r.unsqueeze(1), denom[:, one, :]))
                        link(*(nc.vector.tensor_scalar(work[:, 2, j:j + 1, h * DK:(h + 1) * DK],
                                                            hidden[:, one, h * DK:(h + 1) * DK],
                                                            r[:, h:h + 1], None, ALU.mult) for h in range(HEADS)))
                    nc.vector.tensor_scalar(work[:, 0, :, :], att, 0.0, None, ALU.min).then_inc(elu_in, 1)
                    dve.wait_ge(elu_exp, q + 1)
                    link(nc.vector.scalar_tensor_tensor(out=att, in0=att, scalar=0.0, in1=work[:, 1, :, :],
                                                             op0=ALU.max, op1=ALU.add))
                    link(nc.vector.scalar_tensor_tensor(out=att, in0=att, scalar=-1.0,
                                                             in1=x_sb[:, bass.ds(TILES * q, TILES), :],
                                                             op0=ALU.add, op1=ALU.add))
                    link(*(nc.vector.bn_stats(stats[:, j, :], work[:, 2, j, :]) for j in range(TILES)))
                    dve.sem_inc(vec_gate, 1)
                    link(*(nc.vector.bn_aggr(moments[:, j, :], stats[:, j, :]) for j in range(TILES)))
                    nc.vector.tensor_scalar(powers[:, 0, 0:TILES], moments[:, :, 1], EPS, None,
                                            ALU.add).then_inc(pow_in, 1)
                    nc.vector.tensor_scalar(powers[:, 0, TILES:2 * TILES], degree[:, bass.ds(TILES * q, TILES)], 1.0,
                                            None, ALU.add).then_inc(pow_in, 1)
                    dve.wait_ge(pow_out, q + 1)
                    for j in range(TILES):
                        one = bass.ds(TILES * q + j, 1)
                        mark(nc.vector.tensor_scalar(hidden[:, one, :], work[:, 2, j:j + 1, :],
                                                             moments[:, j, 0:1], powers[:, 1, j:j + 1],
                                                             ALU.subtract, ALU.mult))
                    link(nc.vector.tensor_copy(dis[:, bass.ds(TILES * q, TILES)], powers[:, 1, TILES:2 * TILES]))
                    for j in range(TILES):
                        one = bass.ds(TILES * q + j, 1)
                        nc.vector.tensor_scalar(scaled[:, one, :], hidden[:, one, :], powers[:, 1, TILES + j:TILES + j + 1],
                                                None, ALU.mult).then_inc(scaled_ready, 1)
                    dve.wait_ge(scaled_ready, TILES * q + TILES)
                    assert taken() == PER

                PER = 1 + 3 * TILES
                with dve.Fori(0, PANELS) as q:
                    mark, settle, link, taken = counter(dve, vec_two, PER, q)
                    dve.wait_ge(panel_loaded, 16 * q + 16)
                    for j in range(TILES):
                        d = panel[:, bass.ds(TILES * q + j, 1), j * P:(j + 1) * P]
                        nc.vector.tensor_tensor(d, d, two_ident[:].unsqueeze(1), ALU.add).then_inc(diag_added, 1)
                    dve.wait_ge(lin_done, q + 1)
                    link(*(nc.vector.scalar_tensor_tensor(
                        out=work[:, 0, j, :], in0=ps[:, 6, j * D:(j + 1) * D], scalar=dis[:, bass.ds(TILES * q + j, 1)],
                        in1=bias_sb[:], op0=ALU.mult, op1=ALU.add) for j in range(TILES)))
                    link(nc.vector.scalar_tensor_tensor(out=work[:, 1, :, :], in0=work[:, 0, :, :], scalar=0.0,
                                                             in1=hidden[:, bass.ds(TILES * q, TILES), :],
                                                             op0=ALU.max, op1=ALU.add))
                    link(*(nc.vector.bn_stats(stats[:, j, :], work[:, 1, j, :]) for j in range(TILES)))
                    dve.sem_inc(vec_gate, 1)
                    link(*(nc.vector.bn_aggr(moments[:, j, :], stats[:, j, :]) for j in range(TILES)))
                    nc.vector.tensor_scalar(powers[:, 0, 0:TILES], moments[:, :, 1], EPS, None,
                                            ALU.add).then_inc(pow2_in, 1)
                    dve.wait_ge(pow2_out, q + 1)
                    dve.wait_ge(out_free, q + 1)
                    for j in range(TILES):
                        nc.vector.tensor_scalar(work[:, 2, j, :], work[:, 1, j, :], moments[:, j, 0:1],
                                                powers[:, 1, j:j + 1], ALU.subtract, ALU.mult).then_inc(out_ready, 1)
                    dve.wait_ge(out_ready, TILES * q + TILES)
                    assert taken() == PER

        @block.tensor
        def _(pe):
            with pe.If(pe.value_load(flag[0:1, 0:1]) != 0):
                pe.sem_inc(scores_free, 2)
                pe.sem_inc(group_summed, 8)
                pe.wait_ge(a_ready, 1 + 2 * HEADS)
                nc.tensor.matmul(ps[:, 5, 0:2 * HEADS], lhsT=w0_sb[:], rhs=a_heads[:], start=True,
                                 stop=True).then_inc(score_w_done, 1)
                pe.wait_ge(constants, 3)
                nc.tensor.matmul(ps[:, 6, 0:D], lhsT=ones[0:1, :], rhs=bias_row[:], start=True,
                                 stop=True).then_inc(bias_done, 1)
                pe.wait_ge(proj_w_ready, 1)
                for t in range(BLOCKS):
                    if t >= 4:
                        pe.wait_ge(proj_saved, t - 3)
                    nc.tensor.matmul(ps[:, t % 4, 0:TAB], lhsT=x_t[:, t * P:(t + 1) * P], rhs=proj_w[:], start=True,
                                     stop=True).then_inc(proj_done, 1)
                pe.wait_ge(score_w_ready, HEADS + 2)
                for h in range(HEADS):
                    with pe.Fori(0, N // BANK) as c:
                        pe.wait_ge(rbc_saved, h * (N // BANK) + c + 1)
                        nc.tensor.matmul(ps[:, 7, :], lhsT=score_w[:, h, :], rhs=x_t[:, bass.ds(c * BANK, BANK)],
                                         start=True, stop=True).then_inc(rbc_done, 1)
                with pe.Fori(0, BLOCKS) as t:
                    for h in range(HEADS):
                        pe.wait_ge(probs_ready, HEADS * t + h + 1)
                        for g in range(8):
                            pe.wait_ge(transposed_saved, (HEADS * t + h) * 8 + g + 1)
                            for b in range(4):
                                ins = nc.tensor.transpose(ps[:, g % 4, b * P:(b + 1) * P],
                                                          scores[:, h % 2, (4 * g + b) * P:(4 * g + b + 1) * P], ident[:])
                            ins.then_inc(transposed, 1)
                        if h == 0:
                            pe.wait_ge(sums_saved, t + 1)
                        for g in range(8):
                            pe.wait_ge(transposed_saved, (HEADS * t + h) * 8 + g + 5)
                            for b in range(4 * g, 4 * g + 4):
                                ins = nc.tensor.matmul(ps[:, 4, h * DK:(h + 1) * DK], lhsT=probs_t[:, b, :],
                                                       rhs=table[:, b, h * DK:(h + 1) * DK], start=(b == 0),
                                                       stop=(b == BLOCKS - 1))
                            ins.then_inc(group_summed, 1)
                        pe.wait_ge(group_summed, (HEADS * t + h) * 8 + 16)
                        pe.sem_inc(scores_free, 1)
                    pe.sem_inc(sums_done, 1)
                pe.wait_ge(scaled_ready, BLOCKS)
                with pe.Fori(0, PANELS) as q:
                    pe.wait_ge(diag_added, TILES * q + TILES)
                    for b in range(BLOCKS):
                        ins = nc.tensor.matmul(ps[:, 5, 0:ROWS], lhsT=scaled[:, b, :], rhs=panel[:, b, :], start=(b == 0),
                                               stop=(b == BLOCKS - 1))
                    ins.then_inc(panel_summed, 1)
                    pe.wait_ge(agg_saved, q + 1)
                    for j in range(TILES):
                        ins = nc.tensor.matmul(ps[:, 6, j * D:(j + 1) * D], lhsT=panel_agg[:, j * P:(j + 1) * P],
                                               rhs=w1_sb[:], start=True, stop=True)
                    ins.then_inc(lin_done, 1)


def build(nc, consts, line, x_rows, x_cols, adj, adj_cols, w0, w0_t, a_l, a_r, w1_t, bias, out):
    table_rows = nc.dram_tensor("table_rows", (N, TAB), F32, kind="Internal").ap()
    scaled_rows = nc.dram_tensor("scaled_rows", (N, D), F32, kind="Internal").ap()
    with nc.sbuf_tensor("flag", [1, 1], I32) as flag:
        sparse_path(nc, flag, table_rows, scaled_rows, consts, line, x_rows, adj_cols, w0, w0_t, a_l, a_r, w1_t,
                    bias, out)
        general_path(nc, flag, x_rows, x_cols, adj, adj_cols, w0, w0_t, a_l, a_r, w1_t, bias, out)


def layout_constants(np):
    c = np.zeros((P, CONSTS), np.float32)
    p = np.arange(P)
    c[:, C_IDENT:C_BEFORE] = np.eye(P)
    c[:, C_BEFORE:C_PACK] = p[:, None] < p
    c[p, C_PACK + p // BITS] = 2.0 ** (p % BITS)
    c[:, C_ROWS:C_EDGES] = 1 + np.arange(ROWS)
    c[:, C_EDGES:CONSTS] = 1 + 2 * np.arange(CHUNKS * P)
    c[:, C_PLACE:C_SLOT] = P * np.arange(CHUNKS) + p[:, None]
    c[:, C_SLOT:C_ROW] = np.arange(SLOTS)
    c[:, C_ROW:C_ROW + BLOCKS] = P * (np.arange(BLOCKS) % TILES)
    c[:, C_ROW + BLOCKS:C_BASE] = 1 + p[:, None]
    c[:, C_BASE:C_LOW] = ROWS * np.arange(PANELS)
    for t in range(BLOCKS):
        c[:, C_LOW + t] = P * WINDOW[t % TILES][0]
        c[:, C_HIGH + t] = P * WINDOW[t % TILES][1]
    return c


def kernel(x, adj, L0_gnn_W, L0_gnn_a_l, L0_gnn_a_r, L1_gnn_W, L1_gnn_b):
    import numpy as np
    import concourse.bacc as bacc
    from concourse.bass_utils import run_bass_kernel_spmd

    x, adj = np.asarray(x), np.asarray(adj)
    consts = layout_constants(np)
    arrays = {
        "consts": consts[:, 0:C_ROWS],
        "line": consts[0:1, C_ROWS:CONSTS],
        "x_rows": x,
        "x_cols": x.T,
        "adj": adj,
        "adj_cols": adj.reshape(PANELS, ROWS, BLOCKS, P).transpose(0, 3, 2, 1),
        "w0": np.asarray(L0_gnn_W),
        "w0_t": np.asarray(L0_gnn_W).T,
        "a_l": np.asarray(L0_gnn_a_l).reshape(D, 1),
        "a_r": np.asarray(L0_gnn_a_r).reshape(D, 1),
        "w1_t": np.asarray(L1_gnn_W).T,
        "bias": np.asarray(L1_gnn_b).reshape(1, D),
    }
    arrays = {name: np.ascontiguousarray(a) for name, a in arrays.items()}
    nc = bacc.Bacc("TRN2", target_bir_lowering=False, num_devices=1)
    args = [nc.dram_tensor(name, a.shape, F32, kind="ExternalInput").ap() for name, a in arrays.items()]
    args.append(nc.dram_tensor("out", (N, D), F32, kind="ExternalOutput").ap())
    build(nc, *args)
    return run_bass_kernel_spmd(nc, [arrays], core_ids=[0]).results[0]["out"]
```
